# Optimizing a Trainium2 kernel written in Bass

```python
import numpy as np
import jax
import jax.numpy as jnp

def _softmax(x, axis=-1):
    return jax.nn.softmax(x, axis=axis)

def _gelu(x):
    return jax.nn.gelu(x, approximate=True)

def _silu(x):
    return jax.nn.silu(x)

def _sigmoid(x):
    return jax.nn.sigmoid(x)

def _layernorm(x, axis=-1, eps=1e-05):
    m = jnp.mean(x, axis=axis, keepdims=True)
    v = jnp.var(x, axis=axis, keepdims=True)
    return (x - m) / jnp.sqrt(v + eps)

def _scatter_add(tgt, idx, src, axis=0):
    return tgt.at[idx].add(src)

def _segment_sum(src, seg, n):
    return jax.ops.segment_sum(src, seg, n)
kernel_name = 'mk_adaln_d1_jaxref_r8_f3fc06'

def setup_inputs(seed: int=0):
    np.random.seed(seed)
    _w = jnp.asarray

    def _L0_attn_setup():
        import jax, jax.numpy as jnp
        import numpy as np
        D = 128
        M = 16
        H = D // M
        EPS = 1e-05

        def _rmsnorm(x, w, eps=EPS):
            var = jnp.mean(jnp.square(x), axis=-1, keepdims=True)
            return x * jax.lax.rsqrt(var + eps) * w
        key = jax.random.key(seed)
        ks = jax.random.split(key, 5)
        B, T = (4, 128)
        x = jax.random.normal(ks[0], (B, T, D), dtype=jnp.float32)
        norm_w = jnp.ones((D,), dtype=jnp.float32)
        s = 1.0 / np.sqrt(D)
        W_v = jax.random.uniform(ks[1], (D, D), dtype=jnp.float32, minval=-s, maxval=s)
        W_a = jax.random.uniform(ks[2], (H * M * (M + 1), D), dtype=jnp.float32, minval=-s, maxval=s)
        W_out = jax.random.uniform(ks[3], (D, D), dtype=jnp.float32, minval=-s, maxval=s)
        return {'x': x, 'norm_w': norm_w, 'W_v': W_v, 'W_a': W_a, 'W_out': W_out}
    _L0_attn_in = _L0_attn_setup()

    def _L0_ffn_setup():
        import jax, jax.numpy as jnp
        import numpy as np
        SWIGLU_ALPHA = 1.702
        SWIGLU_LIMIT = 7.0
        TOP_K = 4
        key = jax.random.key(seed)
        k = jax.random.split(key, 5)
        B, S, D, E, I = (2, 128, 128, 8, 256)
        return {'hidden_states': jax.random.normal(k[0], (B, S, D), dtype=jnp.float32), 'router_weight': jax.random.normal(k[1], (E, D), dtype=jnp.float32) * 0.02, 'router_bias': jnp.zeros((E,), dtype=jnp.float32), 'gate_up_proj': jax.random.normal(k[2], (E, 2 * I, D), dtype=jnp.float32) * 0.02, 'gate_up_proj_bias': jnp.zeros((E, 2 * I), dtype=jnp.float32), 'down_proj': jax.random.normal(k[3], (E, D, I), dtype=jnp.float32) * 0.02, 'down_proj_bias': jnp.zeros((E, D), dtype=jnp.float32)}
    _L0_ffn_in = _L0_ffn_setup()
    _L0_c = _w((lambda *s: np.random.randn(*s).astype(np.float32) * 0.05)(8, 128))
    _L0_wmod = _w((lambda *s: np.random.randn(*s).astype(np.float32) * 0.05)(128, 6 * 128) * 128 ** (-0.5))
    _d = {'L0_attn_x': _L0_attn_in['x'], 'L0_attn_norm_w': _L0_attn_in['norm_w'], 'L0_attn_W_v': _L0_attn_in['W_v'], 'L0_attn_W_a': _L0_attn_in['W_a'], 'L0_attn_W_out': _L0_attn_in['W_out'], 'L0_ffn_router_weight': _L0_ffn_in['router_weight'], 'L0_ffn_router_bias': _L0_ffn_in['router_bias'], 'L0_ffn_gate_up_proj': _L0_ffn_in['gate_up_proj'], 'L0_ffn_gate_up_proj_bias': _L0_ffn_in['gate_up_proj_bias'], 'L0_ffn_down_proj': _L0_ffn_in['down_proj'], 'L0_ffn_down_proj_bias': _L0_ffn_in['down_proj_bias'], 'L0_c': _L0_c, 'L0_wmod': _L0_wmod}
    _x0 = _d['L0_attn_x']
    _d['L0_attn_x'] = jax.random.normal(jax.random.fold_in(jax.random.key(seed), 1), (8, 512, 128), dtype=_x0.dtype)
    del _x0
    return _d

def reference(L0_attn_x, L0_attn_norm_w, L0_attn_W_v, L0_attn_W_a, L0_attn_W_out, L0_ffn_router_weight, L0_ffn_router_bias, L0_ffn_gate_up_proj, L0_ffn_gate_up_proj_bias, L0_ffn_down_proj, L0_ffn_down_proj_bias, L0_c, L0_wmod):

    def _L0_attn_ref(x, norm_w, W_v, W_a, W_out):
        import jax, jax.numpy as jnp
        import numpy as np
        D = 128
        M = 16
        H = D // M
        EPS = 1e-05

        def _rmsnorm(x, w, eps=EPS):
            var = jnp.mean(jnp.square(x), axis=-1, keepdims=True)
            return x * jax.lax.rsqrt(var + eps) * w
        B, T, _ = x.shape
        h = _rmsnorm(x, norm_w)
        v = (h @ W_v.T).reshape(B, T, H, M)
        gate_logits = (h @ W_a.T).reshape(B, T, H, M, M + 1)
        gates = jax.nn.softmax(gate_logits, axis=-1)
        a0 = gates[..., 0]
        A = gates[..., 1:]
        A_t = jnp.moveaxis(A, 1, 0)
        u_t = jnp.moveaxis(a0 * v, 1, 0)

        def step(state, inp):
            At, ut = inp
            new = jnp.einsum('bhij,bhj->bhi', At, state) + ut
            return (new, new)
        init = jnp.zeros((B, H, M), dtype=x.dtype)
        _, ys = jax.lax.scan(step, init, (A_t, u_t))
        h_out = jnp.moveaxis(ys, 0, 1).reshape(B, T, D)
        return x + h_out @ W_out.T

    def _L0_ffn_ref(hidden_states, router_weight, router_bias, gate_up_proj, gate_up_proj_bias, down_proj, down_proj_bias):
        import jax, jax.numpy as jnp
        import numpy as np
        SWIGLU_ALPHA = 1.702
        SWIGLU_LIMIT = 7.0
        TOP_K = 4
        B, S, D = hidden_states.shape
        E = router_weight.shape[0]
        x = hidden_states.reshape(-1, D)
        N = x.shape[0]
        logits = x @ router_weight.T + router_bias
        topk_logits, topk_idx = jax.lax.top_k(logits, TOP_K)
        topk_w = jax.nn.softmax(topk_logits.astype(jnp.float32), axis=-1)
        combine = jnp.zeros((N, E), dtype=jnp.float32)
        combine = combine.at[jnp.arange(N)[:, None], topk_idx].set(topk_w)
        gate_up = jnp.einsum('nd,ejd->nej', x, gate_up_proj) + gate_up_proj_bias
        gate, up = jnp.split(gate_up, 2, axis=-1)
        gate = jnp.minimum(gate, SWIGLU_LIMIT)
        up = jnp.clip(up, -SWIGLU_LIMIT, SWIGLU_LIMIT)
        act = (up + 1.0) * gate * jax.nn.sigmoid(SWIGLU_ALPHA * gate)
        out = jnp.einsum('nei,edi->ned', act, down_proj) + down_proj_bias
        y = jnp.einsum('ned,ne->nd', out, combine.astype(out.dtype))
        return y.reshape(B, S, D)
    x = L0_attn_x
    mod = (_silu(L0_c) @ L0_wmod).reshape(L0_c.shape[0], 6, 1, -1)
    sa, ca, ga, sb, cb, gb = (mod[:, 0], mod[:, 1], mod[:, 2], mod[:, 3], mod[:, 4], mod[:, 5])
    ga = (2 * (ga >= 0) - 1) * jnp.maximum(jnp.abs(ga), 0.25)
    gb = (2 * (gb >= 0) - 1) * jnp.maximum(jnp.abs(gb), 0.25)
    h = _layernorm(x, axis=-1) * (1 + ca) + sa
    x = x + ga * _L0_attn_ref(h, L0_attn_norm_w, L0_attn_W_v, L0_attn_W_a, L0_attn_W_out)
    h = _layernorm(x, axis=-1) * (1 + cb) + sb
    x = x + gb * _L0_ffn_ref(h, L0_ffn_router_weight, L0_ffn_router_bias, L0_ffn_gate_up_proj, L0_ffn_gate_up_proj_bias, L0_ffn_down_proj, L0_ffn_down_proj_bias)
    return x

_drawn_inputs = setup_inputs


def setup_inputs(seed=0):
    import zlib

    import numpy as np

    out = dict(_drawn_inputs(seed))
    spreads = {'L0_attn_norm_w': (1.0, 0.6),
     'L0_ffn_router_bias': (0.0, 0.8),
     'L0_ffn_gate_up_proj_bias': (0.0, 0.8),
     'L0_ffn_down_proj_bias': (0.0, 0.69)}
    factors = {'L0_attn_W_v': 7.575,
     'L0_attn_W_a': 8.0,
     'L0_attn_W_out': 7.306,
     'L0_ffn_router_weight': 6.153,
     'L0_ffn_gate_up_proj': 8.0,
     'L0_ffn_down_proj': 8.0}
    for name, (base, spread) in spreads.items():
        noise = np.random.default_rng([zlib.crc32(name.encode()), seed]).standard_normal(out[name].shape)
        drawn = base * np.exp(spread * noise) if base else spread * noise
        out[name] = jnp.asarray(drawn.astype(out[name].dtype))
    for name, factor in factors.items():
        out[name] = (out[name] * factor).astype(out[name].dtype)
    return out
```

```python
from contextlib import ExitStack

import concourse.bass as bass
from concourse import mybir

F32 = mybir.dt.float32
ALU = mybir.AluOpType
ACT = mybir.ActivationFunctionType
AX_X = mybir.AxisListType.X

P = 128
EPS = 1e-5
ALPHA = 1.702
LIMIT = 7.0
TOP_K = 4
FLOOR = 0.25
SILU_LIMIT = 11.914 / (1.0 + 2.718281828459045 ** -11.914)


class Event:

    def __init__(self, sem, per):
        self.sem, self.per = sem, per

    def at(self, c, n):
        return c * self.per + n


def is_first(c):
    return isinstance(c, int) and c == 0


def adaln_block(nc, x, norm_w, w_v, w_a, w_out, router_w, router_b, gu_w, gu_b, down_w, down_b, cond, w_mod, out):
    B, T, D = x.shape
    E, I2, _ = gu_w.shape
    I = I2 // 2
    KI = I // P
    HI = D
    M = w_a.shape[0] // D - 1
    H = D // M
    M1 = M + 1
    NG = HI * M1
    NL = NG + D
    TS = P // B
    TILES = 2
    CS = TILES * TS
    NC = T // CS
    N = TILES * P
    HALF = M // 2
    ROW = HALF * M1
    BH = B * H
    LC = 512
    KL = -(-NL // LC)
    STEP_INCS = 4
    CONSTS = 9

    x_t = x.rearrange("b (n t) d -> n b t d", t=TS)
    out_t = out.rearrange("b (n t) d -> n b t d", t=TS)
    gate_dram = nc.dram_tensor("gate_dram", [TILES, B, H * 2, TS, ROW], F32, kind="Internal").ap()
    y_dram = nc.dram_tensor("y_dram", [TILES, B, H, TS, M], F32, kind="Internal").ap()

    with ExitStack() as ctx:
        def sb(name, shape):
            return ctx.enter_context(nc.sbuf_tensor(name, shape, F32))

        def sem(name):
            return ctx.enter_context(nc.semaphore(name))

        def event(name, per):
            return Event(sem(name), per)

        wa_rows = sb("wa_rows", [P, M1, D])
        gu_rows = sb("gu_rows", [P, E * 2 * KI, D])
        dn_rows = sb("dn_rows", [P, E, I])
        wv_rows = sb("wv_rows", [P, D])
        wo_rows = sb("wo_rows", [P, D])
        rw_rows = sb("rw_rows", [E, D])
        gub_rows = sb("gub_rows", [E * 2 * KI, P])
        c_rows = sb("c_rows", [B, D])
        c_tmp = sb("c_tmp", [B, 3, D])
        c_col = sb("c_col", [P, B])
        c_tok = sb("c_tok", [P, P])
        wmod_sb = sb("wmod_sb", [P, 6 * D])
        nw = sb("nw", [P, 1])
        nws = sb("nws", [P, 1])
        wl = sb("wl", [P, NL])
        wgu = sb("wgu", [P, E, I2])
        wd = sb("wd", [P, E, KI, D])
        wo = sb("wo", [P, D])
        rw = sb("rw", [P, E])
        bgu = sb("bgu", [P, E, 2 * KI])
        bd = sb("bd", [E, D])
        rb = sb("rb", [P, E])
        mod = sb("mod", [P, 6, D])
        g_abs = sb("g_abs", [P, D])
        ident = sb("ident", [P, P])
        lower = sb("lower", [P, E, E])
        minus_half = sb("minus_half", [P, 1])
        eps_mean = sb("eps_mean", [P, 1])
        eps_sum = sb("eps_sum", [P, 1])
        xg = sb("xg", [P, TILES, D])
        st1 = sb("st1", [P, TILES, 6])
        mv1 = sb("mv1", [P, TILES, 2])
        ve1 = sb("ve1", [P, TILES, 1])
        rs1 = sb("rs1", [P, TILES, 1])
        xh = sb("xh", [P, TILES, D])
        hh = sb("hh", [P, TILES, D])
        res = sb("res", [P, TILES, D])
        sq_junk = sb("sq_junk", [P, TILES, D])
        ms = sb("ms", [P, TILES, 1])
        me = sb("me", [P, TILES, 1])
        rms = sb("rms", [P, TILES, 1])
        ht = sb("ht", [P, N])
        lg = sb("lg", [P, TILES, NG])
        vv = sb("vv", [P, TILES, HI])
        nmax = sb("nmax", [P, TILES, HI])
        ex = sb("ex", [P, TILES, NG])
        zs = sb("zs", [P, TILES, HI])
        rz = sb("rz", [P, TILES, HI])
        rv = sb("rv", [P, TILES, HI])
        gates = sb("gates", [P, CS, ROW])
        state = sb("state", [P, CS, M1])
        prod = sb("prod", [P, ROW])
        yt_tok = sb("yt_tok", [P, TILES, HI])
        yt = sb("yt", [P, N])
        r_in = sb("r_in", [P, TILES, D])
        go = sb("go", [P, TILES, D])
        xn = sb("xn", [P, TILES, D])
        st2 = sb("st2", [P, TILES, 6])
        mv2 = sb("mv2", [P, TILES, 2])
        ve2 = sb("ve2", [P, TILES, 1])
        rs2 = sb("rs2", [P, TILES, 1])
        xh2 = sb("xh2", [P, TILES, D])
        h2 = sb("h2", [P, TILES, D])
        h2t = sb("h2t", [P, N])
        rl = sb("rl", [P, TILES, E])
        rmx = sb("rmx", [P, TILES])
        rgt = sb("rgt", [P, TILES, E, E])
        req = sb("req", [P, TILES, E, E])
        rank = sb("rank", [P, TILES, E])
        chosen = sb("chosen", [P, TILES, E])
        rdl = sb("rdl", [P, TILES, E])
        rex = sb("rex", [P, TILES, E])
        rsl = sb("rsl", [P, TILES, E])
        rsum = sb("rsum", [P, TILES])
        rrec = sb("rrec", [P, TILES])
        comb = sb("comb", [P, TILES, E])
        combt = sb("combt", [E, N])
        sg = sb("sg", [P, 2, KI * N])
        up = sb("up", [P, 2, KI * N])
        act_t = sb("act_t", [P, 2, KI * N])
        yacc = sb("yacc", [P, TILES, D])
        gy = sb("gy", [P, TILES, D])
        res_out = sb("res_out", [P, TILES, D])

        ps = ctx.enter_context(nc.psum_tensor("ps", [P, 8, 512], F32))

        def gu_ps(e, which):
            return ps[:, 2 + 2 * (e % 2) + which, :]

        def bank_a(j):
            return ps[:, 6, j * P:(j + 1) * P]

        def bank_b(j):
            return ps[:, 7, j * P:(j + 1) * P]

        in_c, in_wmod, in_nw, in_wa = sem("in_c"), sem("in_wmod"), sem("in_nw"), sem("in_wa")
        in_small, in_gu, in_dn = sem("in_small"), sem("in_gu"), sem("in_dn")
        consts = sem("consts")
        passed_sp, passed_pool, passed_dve = sem("passed_sp"), sem("passed_pool"), sem("passed_dve")
        c_step = sem("c_step")
        c_t, nws_ok = sem("c_t"), sem("nws_ok")
        mod_ps, mod_step = sem("mod_ps"), sem("mod_step")
        mod_ready = sem("mod_ready")
        w_ps, w_ev_act, w_ev_dve = sem("w_ps"), sem("w_ev_act"), sem("w_ev_dve")
        x_in = [event(f"x_in{j}", 16) for j in range(TILES)]
        st1_ok, mv1_ok = event("st1_ok", TILES), event("mv1_ok", TILES)
        ve1_ok, rs1_ok = event("ve1_ok", TILES), event("rs1_ok", TILES)
        xh_ok, hm_ok, h_ok = event("xh_ok", TILES), event("hm_ok", TILES), event("h_ok", TILES)
        gh_ok, res_ok = event("gh_ok", TILES), event("res_ok", TILES)
        res_st = [event(f"res_st{j}", 16) for j in range(TILES)]
        ms_ok, me_ok, rms_ok = event("ms_ok", TILES), event("me_ok", TILES), event("rms_ok", TILES)
        ht_ps, ht_ok = event("ht_ps", 1), event("ht_ok", 1)
        lg_ps, lg_ev = event("lg_ps", TILES * KL), event("lg_ev", TILES * KL)
        nmax_ok = event("nmax_ok", TILES)
        sub_ok = event("sub_ok", TILES)
        exp_ok = event("exp_ok", TILES)
        zs_ok, rz_ok, rv_ok = event("zs_ok", TILES), event("rz_ok", TILES), event("rv_ok", TILES)
        norm_ok = event("norm_ok", 2 * TILES)
        g_st = [event(f"g_st{j}", 16 * B) for j in range(TILES)]
        g_ld = [event(f"g_ld{j}", 32) for j in range(TILES)]
        scan = event("scan", STEP_INCS * CS)
        y_st = [event(f"y_st{j}", 16) for j in range(TILES)]
        y_ld = [event(f"y_ld{j}", 16 * B) for j in range(TILES)]
        yt_ps, yt_ok, o_ps = event("yt_ps", 1), event("yt_ok", 1), event("o_ps", 1)
        r_ld = [event(f"r_ld{j}", 16) for j in range(TILES)]
        go_ok, xn_ok = event("go_ok", TILES), event("xn_ok", TILES)
        st2_ok, mv2_ok = event("st2_ok", TILES), event("mv2_ok", TILES)
        ve2_ok, rs2_ok = event("ve2_ok", TILES), event("rs2_ok", TILES)
        xh2_ok, hm2_ok, h2_ok = event("xh2_ok", TILES), event("hm2_ok", TILES), event("h2_ok", TILES)
        h2t_ps, h2t_ok = event("h2t_ps", 1), event("h2t_ok", 1)
        r_ps = event("r_ps", 1)
        route = event("route", 11)
        rex_ok = event("rex_ok", 1)
        comb_ok = event("comb_ok", 1)
        combt_ps, combt_ok, b_ps = event("combt_ps", 1), event("combt_ok", 1), event("b_ps", 1)
        bias_ok = event("bias_ok", 1)
        gu_done = event("gu_done", 2 * E)
        sg_ok, up_ok = event("sg_ok", E), event("up_ok", E)
        clamp_ok = event("clamp_ok", E)
        act_ok = event("act_ok", E)
        dn_done = event("dn_done", E)
        acc_ok = event("acc_ok", TILES * E)
        gy_ok, ro_ok = event("gy_ok", TILES), event("ro_ok", TILES)
        out_st = [event(f"out_st{j}", 16) for j in range(TILES)]

        block = ctx.enter_context(nc.Block())

        def whole(run):
            FULL = 4
            for it in range(FULL):
                run(it, it - 1 if it >= 1 else None, it - 2 if it >= 2 else None, it - 3 if it >= 3 else None)
            yield FULL, NC
            for it in range(NC, NC + 3):
                run(None, it - 1 if it < NC + 1 else None, it - 2 if it < NC + 2 else None, it - 3)

        WA_GROUPS = [(1, 4), (5, 4), (9, 4), (13, 4)]
        N_WA = 1 + len(WA_GROUPS)
        N_GROUPS = N_WA + E + E * KI // 4 + 1

        def wl_dst(j0, n, half):
            if half == 0 or j0 == 0:
                to = j0
            else:
                to = (j0 - 1 + HALF) % M + 1
            v = wl[:, 0:NG].rearrange("p (h g i j) -> p j h g i", h=H, g=2, i=HALF)
            return v[:, to:to + n, :, half, :]

        def wl_src(bank, n, half):
            v = ps[:, bank, 0:n * P].rearrange("p (j h g i) -> p j h g i", j=n, h=H, g=2)
            return v[:, :, :, half, :]

        @block.sync
        def _(sp):
            sp.dma_start(c_rows[:, :], cond).then_inc(in_c, 16)
            sp.dma_start(wmod_sb[:, :], w_mod).then_inc(in_wmod, 16)
            sp.dma_start(nw[:, :], norm_w.rearrange("(d o) -> d o", o=1)).then_inc(in_nw, 16)
            sp.dma_start(wa_rows[:, :, :], w_a.rearrange("(r j) d -> r j d", j=M1)).then_inc(in_wa, 16)
            sp.dma_start(wv_rows[:, :], w_v).then_inc(in_small, 16)
            sp.dma_start(wo_rows[:, :], w_out).then_inc(in_small, 16)
            sp.dma_start(rw_rows[:, :], router_w).then_inc(in_small, 16)
            sp.dma_start(gub_rows[:, :], gu_b.rearrange("e (k p) -> (e k) p", p=P)).then_inc(in_small, 16)
            sp.dma_start(bd[:, :], down_b).then_inc(in_small, 16)
            sp.dma_start(rb[:, :], router_b.partition_broadcast(P)).then_inc(in_small, 16)

            def run(g, e, s, m):
                for j in range(TILES):
                    if g is not None:
                        if not is_first(g):
                            sp.wait_ge(res_ok.sem, res_ok.at(g - 1, j + 1))
                            sp.sem_inc(passed_sp, 1)
                        sp.dma_start(xg[:, j, :], x_t[2 * g + j]).then_inc(x_in[j].sem, 16)
                    if m is not None:
                        sp.wait_ge(res_st[j].sem, res_st[j].at(m, 16))
                        sp.sem_inc(passed_sp, 1)
                        if not is_first(m):
                            sp.wait_ge(xn_ok.sem, xn_ok.at(m - 1, j + 1))
                            sp.sem_inc(passed_sp, 1)
                        sp.dma_start(r_in[:, j, :], out_t[2 * m + j]).then_inc(r_ld[j].sem, 16)
                if isinstance(g, int) and g == 0:
                    sp.dma_start(gu_rows[:, :, :], gu_w.rearrange("e (k p) d -> p (e k) d", p=P)).then_inc(in_gu, 16)
                    sp.dma_start(dn_rows[:, :, :], down_w.rearrange("e d i -> d e i")).then_inc(in_dn, 16)
                if g is not None:
                    for j in range(TILES):
                        sp.wait_ge(res_ok.sem, res_ok.at(g, j + 1))
                        sp.sem_inc(passed_sp, 1)
                        sp.dma_start(out_t[2 * g + j], res[:, j, :]).then_inc(res_st[j].sem, 16)
                for j in range(TILES):
                    if e is not None:
                        sp.wait_ge(norm_ok.sem, norm_ok.at(e, 2 * j + 2))
                        sp.sem_inc(passed_sp, 1)
                        if not is_first(e):
                            sp.wait_ge(g_ld[j].sem, g_ld[j].at(e, 0))
                            sp.sem_inc(passed_sp, 1)
                        for b in range(B):
                            sp.dma_start(gate_dram[j, b].rearrange("r t e -> t r e"),
                                         ex[b * TS:(b + 1) * TS, j, :].rearrange("p (r e) -> p r e", e=ROW)
                                         ).then_inc(g_st[j].sem, 16)
                    if s is not None:
                        sp.wait_ge(scan.sem, scan.at(s, STEP_INCS * TS * (j + 1)))
                        sp.sem_inc(passed_sp, 1)
                        if not is_first(s):
                            sp.wait_ge(y_ld[j].sem, y_ld[j].at(s, 0))
                            sp.sem_inc(passed_sp, 1)
                        sp.dma_start(y_dram[j].rearrange("b h t i -> (b h) t i"),
                                     state[0:BH, j * TS:(j + 1) * TS, 1:M1]).then_inc(y_st[j].sem, 16)
                    if e is not None:
                        sp.wait_ge(g_st[j].sem, g_st[j].at(e, 16 * B))
                        sp.sem_inc(passed_sp, 1)
                        for half in range(2):
                            sp.dma_start(gates[half * BH:(half + 1) * BH, j * TS:(j + 1) * TS, :],
                                         gate_dram[j].rearrange("b (h g) t e -> g (b h) t e", g=2)[half]
                                         ).then_inc(g_ld[j].sem, 16)
                    if s is not None:
                        sp.wait_ge(y_st[j].sem, y_st[j].at(s, 16))
                        sp.sem_inc(passed_sp, 1)
                        if not is_first(s):
                            sp.wait_ge(yt_ps.sem, yt_ps.at(s - 1, 1))
                            sp.sem_inc(passed_sp, 1)
                        for b in range(B):
                            sp.dma_start(yt_tok[b * TS:(b + 1) * TS, j, :].rearrange("t (h i) -> t h i", h=H),
                                         y_dram[j, b].rearrange("h t i -> t h i")).then_inc(y_ld[j].sem, 16)
                if m is not None:
                    for j in range(TILES):
                        sp.wait_ge(ro_ok.sem, ro_ok.at(m, j + 1))
                        sp.sem_inc(passed_sp, 1)
                        sp.dma_start(out_t[2 * m + j], res_out[:, j, :]).then_inc(out_st[j].sem, 16)

            for lo, hi in whole(run):
                with sp.Fori(lo, hi) as it:
                    run(it, it - 1, it - 2, it - 3)
            for j in range(TILES):
                sp.wait_ge(out_st[j].sem, out_st[j].at(NC, 0))

        @block.gpsimd
        def _(pool):
            nc.gpsimd.memset(ident[:, :], 0.0).then_inc(consts, 1)
            nc.gpsimd.memset(lower[:, :, :], 1.0).then_inc(consts, 1)
            nc.gpsimd.memset(minus_half[:, :], -0.5).then_inc(consts, 1)
            nc.gpsimd.memset(eps_mean[:, :], EPS).then_inc(consts, 1)
            nc.gpsimd.memset(eps_sum[:, :], EPS * D).then_inc(consts, 1)
            nc.gpsimd.memset(state[:, :, :], 0.0).then_inc(consts, 1)
            pool.wait_ge(consts, 6)
            nc.gpsimd.memset(state[:, :, 0:1], 1.0).then_inc(consts, 1)
            nc.gpsimd.affine_select(out=ident[:, :], in_=ident[:, :], compare_op=ALU.not_equal, fill=1.0, base=0,
                                    pattern=[[-1, P]], channel_multiplier=1).then_inc(consts, 1)
            nc.gpsimd.affine_select(out=lower[:, :, :], in_=lower[:, :, :], compare_op=ALU.is_gt, fill=0.0, base=0,
                                    pattern=[[1, E], [-1, E]], channel_multiplier=0).then_inc(consts, 1)

            def inv_sqrt(src, eps, mid, dst, mid_ok, dst_ok, c, j):
                nc.gpsimd.tensor_tensor(mid[:, j, :], src, eps, ALU.add).then_inc(mid_ok.sem, 1)
                pool.wait_ge(mid_ok.sem, mid_ok.at(c, j + 1))
                nc.gpsimd.tensor_tensor(dst[:, j, :], mid[:, j, :], minus_half[:, :], ALU.pow).then_inc(dst_ok.sem, 1)

            def norm_gates(e, j, part):
                if part == 0:
                    pool.wait_ge(rv_ok.sem, rv_ok.at(e, j + 1))
                lo, hi = part * HI // 2, (part + 1) * HI // 2
                v = ex[:, j, :].rearrange("p (r k) -> p r k", k=M1)[:, lo:hi, :]
                nc.gpsimd.tensor_tensor(v[:, :, 0], v[:, :, 0], rv[:, j, lo:hi], ALU.mult)
                nc.gpsimd.tensor_tensor(v[:, :, 1:M1], v[:, :, 1:M1],
                                        rz[:, j, lo:hi].unsqueeze(2).broadcast_to([P, HI // 2, M]),
                                        ALU.mult).then_inc(norm_ok.sem, 1)

            def sub_max(g, j):
                pool.wait_ge(nmax_ok.sem, nmax_ok.at(g, j + 1))
                v = lg[:, j, :].rearrange("p (r k) -> p r k", k=M1)
                nc.gpsimd.tensor_tensor(v, v, nmax[:, j, :].unsqueeze(2).broadcast_to([P, HI, M1]),
                                        ALU.add).then_inc(sub_ok.sem, 1)

            def run(g, e, s, m):
                for j in range(TILES):
                    if m is not None:
                        pool.wait_ge(go_ok.sem, go_ok.at(m, j + 1))
                        pool.wait_ge(r_ld[j].sem, r_ld[j].at(m, 16))
                        nc.gpsimd.tensor_tensor(xn[:, j, :], go[:, j, :], r_in[:, j, :], ALU.add).then_inc(xn_ok.sem, 1)
                for j in range(TILES):
                    if g is not None:
                        pool.wait_ge(mv1_ok.sem, mv1_ok.at(g, j + 1))
                        inv_sqrt(mv1[:, j, 1:2], eps_mean[:, :], ve1, rs1, ve1_ok, rs1_ok, g, j)
                for j in range(TILES):
                    if m is not None:
                        pool.wait_ge(mv2_ok.sem, mv2_ok.at(m, j + 1))
                        inv_sqrt(mv2[:, j, 1:2], eps_mean[:, :], ve2, rs2, ve2_ok, rs2_ok, m, j)
                for j in range(TILES):
                    if g is not None:
                        if is_first(g) and j == 0:
                            pool.wait_ge(mod_ready, 1)
                        pool.wait_ge(xh_ok.sem, xh_ok.at(g, j + 1))
                        nc.gpsimd.tensor_tensor(hh[:, j, :], xh[:, j, :], mod[:, 1, :], ALU.mult).then_inc(hm_ok.sem, 1)
                        pool.wait_ge(hm_ok.sem, hm_ok.at(g, j + 1))
                        nc.gpsimd.tensor_tensor(hh[:, j, :], hh[:, j, :], mod[:, 0, :], ALU.add).then_inc(h_ok.sem, 1)
                for j in range(TILES):
                    if m is not None:
                        pool.wait_ge(xh2_ok.sem, xh2_ok.at(m, j + 1))
                        nc.gpsimd.tensor_tensor(h2[:, j, :], xh2[:, j, :], mod[:, 4, :], ALU.mult).then_inc(hm2_ok.sem, 1)
                        pool.wait_ge(hm2_ok.sem, hm2_ok.at(m, j + 1))
                        nc.gpsimd.tensor_tensor(h2[:, j, :], h2[:, j, :], mod[:, 3, :], ALU.add).then_inc(h2_ok.sem, 1)
                for j in range(TILES):
                    if g is not None:
                        pool.wait_ge(ms_ok.sem, ms_ok.at(g, j + 1))
                        inv_sqrt(ms[:, j, :], eps_sum[:, :], me, rms, me_ok, rms_ok, g, j)
                for j in range(TILES):
                    if g is not None:
                        if not is_first(g):
                            pool.wait_ge(res_st[j].sem, res_st[j].at(g, 0))
                        pool.wait_ge(h_ok.sem, h_ok.at(g, j + 1))
                        nc.gpsimd.tensor_tensor(res[:, j, :], hh[:, j, :], mod[:, 2, :], ALU.mult).then_inc(gh_ok.sem, 1)
                        pool.wait_ge(gh_ok.sem, gh_ok.at(g, j + 1))
                        nc.gpsimd.tensor_tensor(res[:, j, :], res[:, j, :], xg[:, j, :], ALU.add).then_inc(res_ok.sem, 1)
                for k in range(E):
                    if e is not None and k < 4:
                        norm_gates(e, k // 2, k % 2)
                    if m is not None:
                        pool.wait_ge(up_ok.sem, up_ok.at(m, k + 1))
                        pool.sem_inc(passed_pool, 1)
                        nc.gpsimd.tensor_scalar(up[:, k % 2, :], up[:, k % 2, :], 1.0 + LIMIT, 1.0 - LIMIT,
                                                ALU.min, ALU.max).then_inc(clamp_ok.sem, 1)
                    if g is not None and k in (5, 7):
                        sub_max(g, (k - 5) // 2)
                for j in range(TILES):
                    if m is not None:
                        if not is_first(m):
                            pool.wait_ge(out_st[j].sem, out_st[j].at(m, 0))
                        pool.wait_ge(acc_ok.sem, acc_ok.at(m, TILES * (E - 1) + j + 1))
                        nc.gpsimd.tensor_tensor(gy[:, j, :], yacc[:, j, :], mod[:, 5, :], ALU.mult).then_inc(gy_ok.sem, 1)
                        pool.wait_ge(gy_ok.sem, gy_ok.at(m, j + 1))
                        nc.gpsimd.tensor_tensor(res_out[:, j, :], gy[:, j, :], xn[:, j, :], ALU.add).then_inc(ro_ok.sem, 1)

            for lo, hi in whole(run):
                with pool.Fori(lo, hi) as it:
                    run(it, it - 1, it - 2, it - 3)

        @block.scalar
        def _(act):
            act.wait_ge(in_c, 16)
            nc.scalar.activation(c_tmp[:, 0, :], c_rows[:, :], ACT.Exp, scale=-1.0).then_inc(c_step, 1)
            for k in range(6):
                act.wait_ge(mod_ps, 2)
                src = ps[:, 6 + k // 4, (k % 4) * P:(k % 4 + 1) * P]
                if k in (1, 4):
                    nc.scalar.activation(mod[:, k, :], src, ACT.Copy, bias=1.0).then_inc(mod_step, 1)
                else:
                    nc.scalar.activation(mod[:, k, :], src, ACT.Copy).then_inc(mod_step, 1)
            act.wait_ge(nws_ok, 1)
            act.wait_ge(w_ps, 1)
            for half in range(2):
                nc.scalar.activation(wl_dst(0, 1, half), wl_src(0, 1, half), ACT.Copy, scale=nws[:, 0:1])
            nc.scalar.activation(wl[:, NG:NL], ps[:, 0, P:2 * P], ACT.Copy, scale=nws[:, 0:1])
            nc.scalar.activation(wo[:, :], ps[:, 0, 2 * P:3 * P], ACT.Copy)
            nc.scalar.activation(rw[:, :], ps[:, 0, 3 * P:3 * P + E], ACT.Copy).then_inc(w_ev_act, 1)
            for n in range(1, N_GROUPS):
                if n % 2:
                    continue
                act.wait_ge(w_ps, n + 1)
                bank = n % 6
                if n < N_WA:
                    for half in range(2):
                        last = nc.scalar.activation(wl_dst(*WA_GROUPS[n - 1], half), wl_src(bank, 4, half), ACT.Copy,
                                                    scale=nws[:, 0:1])
                elif n < N_WA + E:
                    last = nc.scalar.activation(wgu[:, n - N_WA, :], ps[:, bank, :], ACT.Copy)
                elif n < N_GROUPS - 1:
                    q = n - N_WA - E
                    last = nc.scalar.activation(wd[:, 2 * q:2 * q + 2, :, :], ps[:, bank, :], ACT.Copy, scale=1.0 / ALPHA)
                else:
                    v = ps[:, bank, 0:E * 2 * KI].rearrange("p (e k) -> p e k", e=E)
                    nc.scalar.activation(bgu[:, :, 0:KI], v[:, :, 0:KI], ACT.Copy, scale=ALPHA)
                    last = nc.scalar.activation(bgu[:, :, KI:2 * KI], v[:, :, KI:2 * KI], ACT.Copy, bias=1.0)
                last.then_inc(w_ev_act, 1)

            def softmax_exp(e, j):
                act.wait_ge(sub_ok.sem, sub_ok.at(e, j + 1))
                if not is_first(e):
                    act.wait_ge(g_st[j].sem, g_st[j].at(e, 0))
                nc.scalar.activation(ex[:, j, :], lg[:, j, :], ACT.Exp).then_inc(exp_ok.sem, 1)

            def logits_out(g, n):
                j, k = n // KL, n % KL
                if k == 0:
                    act.wait_ge(rms_ok.sem, rms_ok.at(g, j + 1))
                    if not is_first(g):
                        act.wait_ge(exp_ok.sem, exp_ok.at(g - 1, j + 1))
                act.wait_ge(lg_ps.sem, lg_ps.at(g, n + 1))
                bank = n % 2
                if k < KL - 1:
                    nc.scalar.activation(lg[:, j, k * LC:(k + 1) * LC], ps[:, bank, :], ACT.Copy,
                                         scale=rms[:, j, :]).then_inc(lg_ev.sem, 1)
                else:
                    w = NG - k * LC
                    nc.scalar.activation(lg[:, j, k * LC:NG], ps[:, bank, 0:w], ACT.Copy, scale=rms[:, j, :])
                    if not is_first(g):
                        act.wait_ge(rv_ok.sem, rv_ok.at(g - 1, j + 1))
                    nc.scalar.activation(vv[:, j, :], ps[:, bank, w:w + D], ACT.Copy,
                                         scale=rms[:, j, :]).then_inc(lg_ev.sem, 1)

            def run(g, e, s, m):
                if m is not None:
                    act.wait_ge(yt_ps.sem, yt_ps.at(m, 1))
                    nc.scalar.activation(yt[:, :], ps[:, 6, 0:N], ACT.Copy).then_inc(yt_ok.sem, 1)
                if e is not None:
                    softmax_exp(e, 0)
                if g is not None:
                    for j in range(TILES):
                        act.wait_ge(h_ok.sem, h_ok.at(g, j + 1))
                        nc.scalar.activation(sq_junk[:, j, :], hh[:, j, :], ACT.Square,
                                             accum_out=ms[:, j, :]).then_inc(ms_ok.sem, 1)
                    act.wait_ge(ht_ps.sem, ht_ps.at(g, 1))
                    nc.scalar.activation(ht[:, :], ps[:, 6, 0:N], ACT.Copy).then_inc(ht_ok.sem, 1)
                if e is not None:
                    softmax_exp(e, 1)
                if m is not None:
                    act.wait_ge(h2t_ps.sem, h2t_ps.at(m, 1))
                    nc.scalar.activation(h2t[:, :], ps[:, 7, 0:N], ACT.Copy).then_inc(h2t_ok.sem, 1)
                if g is not None:
                    for n in range(KL):
                        logits_out(g, n)
                if m is not None:
                    act.wait_ge(route.sem, route.at(m, 7))
                    nc.scalar.activation(rex[:, :, :], rdl[:, :, :], ACT.Exp).then_inc(rex_ok.sem, 1)
                for k in range(E):
                    if m is not None:
                        act.wait_ge(gu_done.sem, gu_done.at(m, 2 * k + 1))
                        if k >= 2:
                            act.wait_ge(act_ok.sem, act_ok.at(m, k - 1))
                        elif not is_first(m):
                            act.wait_ge(act_ok.sem, act_ok.at(m - 1, E + k - 1))
                        for q in range(KI):
                            last = nc.scalar.activation(sg[:, k % 2, q * N:(q + 1) * N], gu_ps(k, 0)[:, q * N:(q + 1) * N],
                                                        ACT.Silu, bias=bgu[:, k, q:q + 1], scale=ALPHA)
                        last.then_inc(sg_ok.sem, 1)
                        act.wait_ge(gu_done.sem, gu_done.at(m, 2 * k + 2))
                        for q in range(KI):
                            last = nc.scalar.activation(up[:, k % 2, q * N:(q + 1) * N], gu_ps(k, 1)[:, q * N:(q + 1) * N],
                                                        ACT.Identity, bias=bgu[:, k, KI + q:KI + q + 1])
                        last.then_inc(up_ok.sem, 1)
                    if m is not None and k == 0:
                        act.wait_ge(combt_ps.sem, combt_ps.at(m, 1))
                        nc.scalar.activation(combt[:, :], ps[0:E, 6, 0:N], ACT.Copy).then_inc(combt_ok.sem, 1)
                        act.wait_ge(b_ps.sem, b_ps.at(m, 1))
                        if not is_first(m):
                            act.wait_ge(gy_ok.sem, gy_ok.at(m - 1, TILES))
                        nc.scalar.activation(yacc[:, :, :].rearrange("p j d -> p (j d)"), ps[:, 7, 0:N],
                                             ACT.Copy).then_inc(bias_ok.sem, 1)
                    if g is not None and 1 <= k <= KL:
                        logits_out(g, KL + k - 1)

            for lo, hi in whole(run):
                with act.Fori(lo, hi) as it:
                    run(it, it - 1, it - 2, it - 3)

        @block.vector
        def _(dve):
            dve.wait_ge(c_step, 1)
            nc.vector.tensor_scalar(c_tmp[:, 1, :], c_tmp[:, 0, :], 1.0, None, ALU.add).then_inc(c_step, 1)
            dve.wait_ge(c_step, 2)
            nc.vector.reciprocal(c_tmp[:, 2, :], c_tmp[:, 1, :]).then_inc(c_step, 1)
            dve.wait_ge(c_step, 3)
            nc.vector.tensor_tensor(c_rows[:, :], c_rows[:, :], c_tmp[:, 2, :], ALU.mult).then_inc(c_step, 1)
            dve.wait_ge(c_t, 1)
            nc.vector.tensor_copy(c_tok[:, :].rearrange("p (b t) -> p b t", b=B),
                                  ps[:, 5, 0:B].unsqueeze(2).broadcast_to([P, B, TS])).then_inc(c_step, 1)
            done = 6
            for k in (2, 5):
                dve.wait_ge(mod_step, done)
                nc.vector.scalar_tensor_tensor(out=g_abs[:, :], in0=mod[:, k, :], scalar=-1.0, in1=mod[:, k, :],
                                               op0=ALU.mult, op1=ALU.max).then_inc(mod_step, 1)
                done += 1
                dve.wait_ge(mod_step, done)
                nc.vector.tensor_scalar(g_abs[:, :], g_abs[:, :], FLOOR, None, ALU.max).then_inc(mod_step, 1)
                nc.vector.tensor_scalar(mod[:, k, :], mod[:, k, :], 0.0, 2.0, ALU.is_ge, ALU.mult).then_inc(mod_step, 1)
                done += 2
                dve.wait_ge(mod_step, done)
                last = nc.vector.scalar_tensor_tensor(out=mod[:, k, :], in0=mod[:, k, :], scalar=-1.0, in1=g_abs[:, :],
                                                      op0=ALU.add, op1=ALU.mult)
                if k == 2:
                    last.then_inc(mod_step, 1)
                    done += 1
                else:
                    last.then_inc(mod_ready, 1)
            dve.wait_ge(in_nw, 16)
            nc.vector.tensor_scalar(nws[:, :], nw[:, :], float(D) ** 0.5, None, ALU.mult).then_inc(nws_ok, 1)
            dve.wait_ge(nws_ok, 1)
            for n in range(1, N_GROUPS):
                if n % 2 == 0:
                    continue
                dve.wait_ge(w_ps, n + 1)
                bank = n % 6
                if n < N_WA:
                    for half in range(2):
                        last = nc.vector.tensor_scalar(wl_dst(*WA_GROUPS[n - 1], half), wl_src(bank, 4, half),
                                                       nws[:, 0:1], None, ALU.mult)
                elif n < N_WA + E:
                    last = nc.vector.tensor_copy(wgu[:, n - N_WA, :], ps[:, bank, :])
                elif n < N_GROUPS - 1:
                    q = n - N_WA - E
                    last = nc.vector.tensor_scalar(wd[:, 2 * q:2 * q + 2, :, :].rearrange("p e k d -> p (e k d)"),
                                                   ps[:, bank, :], 1.0 / ALPHA, None, ALU.mult)
                else:
                    v = ps[:, bank, 0:E * 2 * KI].rearrange("p (e k) -> p e k", e=E)
                    nc.vector.tensor_scalar(bgu[:, :, 0:KI], v[:, :, 0:KI], ALPHA, None, ALU.mult)
                    last = nc.vector.tensor_scalar(bgu[:, :, KI:2 * KI], v[:, :, KI:2 * KI], 1.0, None, ALU.add)
                last.then_inc(w_ev_dve, 1)
            dve.wait_ge(consts, CONSTS)

            def stats(src, st, mv, st_ok, mv_ok, c, j):
                nc.vector.bn_stats(st[:, j, :], src[:, j, :]).then_inc(st_ok.sem, 1)
                dve.wait_ge(st_ok.sem, st_ok.at(c, j + 1))
                dve.sem_inc(passed_dve, 1)
                nc.vector.bn_aggr(mv[:, j, :], st[:, j, :]).then_inc(mv_ok.sem, 1)

            def normalise(dst, src, mv, rs, rs_ok, dst_ok, c, j):
                dve.wait_ge(rs_ok.sem, rs_ok.at(c, j + 1))
                nc.vector.tensor_scalar(dst[:, j, :], src[:, j, :], mv[:, j, 0:1], rs[:, j, :],
                                        ALU.subtract, ALU.mult).then_inc(dst_ok.sem, 1)

            def row_max(g, j):
                dve.wait_ge(lg_ev.sem, lg_ev.at(g, KL * (j + 1)))
                nc.vector.tensor_reduce(nmax[:, j, :], lg[:, j, :].rearrange("p (r k) -> p r k", k=M1), AX_X, ALU.max,
                                        negate=True).then_inc(nmax_ok.sem, 1)

            def row_sum(e, j):
                dve.wait_ge(exp_ok.sem, exp_ok.at(e, j + 1))
                if not is_first(e):
                    dve.wait_ge(norm_ok.sem, norm_ok.at(e - 1, 2 * j + 2))
                nc.vector.tensor_reduce(zs[:, j, :], ex[:, j, :].rearrange("p (r k) -> p r k", k=M1), AX_X,
                                        ALU.add).then_inc(zs_ok.sem, 1)

            def row_inverse(e, j):
                dve.wait_ge(zs_ok.sem, zs_ok.at(e, j + 1))
                nc.vector.reciprocal(rz[:, j, :], zs[:, j, :]).then_inc(rz_ok.sem, 1)
                dve.wait_ge(rz_ok.sem, rz_ok.at(e, j + 1))
                nc.vector.tensor_tensor(rv[:, j, :], rz[:, j, :], vv[:, j, :], ALU.mult).then_inc(rv_ok.sem, 1)

            def steps(s, lo, hi):
                if s is None:
                    return
                for t in range(lo, hi):
                    if t % TS == 0:
                        j = t // TS
                        dve.wait_ge(g_ld[j].sem, g_ld[j].at(s, 32))
                        if not is_first(s):
                            dve.wait_ge(y_st[j].sem, y_st[j].at(s, 0))
                    before = scan.at(s, STEP_INCS * t)
                    if not (is_first(s) and t == 0):
                        dve.wait_ge(scan.sem, before)
                    nc.vector.tensor_tensor(
                        prod[:, :].rearrange("p (i k) -> p i k", k=M1),
                        gates[:, t, :].rearrange("p (i k) -> p i k", k=M1),
                        state[:, (t - 1) % CS, :].unsqueeze(1).broadcast_to([P, HALF, M1]), ALU.mult).then_inc(scan.sem, 1)
                    dve.wait_ge(scan.sem, before + 1)
                    nc.vector.tensor_reduce(state[:, t, 1:1 + HALF], prod[:, :].rearrange("p (i k) -> p i k", k=M1),
                                            AX_X, ALU.add).then_inc(scan.sem, 1)
                    dve.wait_ge(scan.sem, before + 2)
                    nc.vector.tensor_copy(state[0:BH, t, 1 + HALF:M1],
                                          state[BH:2 * BH, t, 1:1 + HALF]).then_inc(scan.sem, 1)
                    nc.vector.tensor_copy(state[BH:2 * BH, t, 1 + HALF:M1],
                                          state[0:BH, t, 1:1 + HALF]).then_inc(scan.sem, 1)

            def routing(m):
                dve.wait_ge(r_ps.sem, r_ps.at(m, 1))
                nc.vector.tensor_tensor(rl[:, :, :], ps[:, 6, 0:N].rearrange("p (j c) -> p j c", j=TILES)[:, :, 0:E],
                                        rb[:, :].unsqueeze(1).broadcast_to([P, TILES, E]), ALU.add).then_inc(route.sem, 1)
                dve.wait_ge(route.sem, route.at(m, 1))
                nc.vector.tensor_reduce(rmx[:, :], rl[:, :, :], AX_X, ALU.max).then_inc(route.sem, 1)
                other = rl[:, :, :].unsqueeze(2).broadcast_to([P, TILES, E, E])
                own = rl[:, :, :].unsqueeze(3).broadcast_to([P, TILES, E, E])
                nc.vector.tensor_tensor(rgt[:, :, :, :], other, own, ALU.is_gt).then_inc(route.sem, 1)
                nc.vector.tensor_tensor(req[:, :, :, :], other, own, ALU.is_equal).then_inc(route.sem, 1)
                dve.wait_ge(route.sem, route.at(m, 4))
                nc.vector.tensor_tensor(req[:, :, :, :], req[:, :, :, :],
                                        lower[:, :, :].unsqueeze(1).broadcast_to([P, TILES, E, E]), ALU.mult
                                        ).then_inc(route.sem, 1)
                dve.wait_ge(route.sem, route.at(m, 5))
                nc.vector.tensor_tensor(rgt[:, :, :, :], rgt[:, :, :, :], req[:, :, :, :], ALU.add).then_inc(route.sem, 1)
                nc.vector.tensor_tensor(rdl[:, :, :], rl[:, :, :], rmx[:, :].unsqueeze(2).broadcast_to([P, TILES, E]),
                                        ALU.subtract).then_inc(route.sem, 1)
                dve.wait_ge(route.sem, route.at(m, 7))
                nc.vector.tensor_reduce(rank[:, :, :], rgt[:, :, :, :], AX_X, ALU.add).then_inc(route.sem, 1)
                dve.wait_ge(route.sem, route.at(m, 8))
                dve.wait_ge(rex_ok.sem, rex_ok.at(m, 1))
                nc.vector.scalar_tensor_tensor(out=rsl[:, :, :].rearrange("p j e -> p (j e)"),
                                               in0=rank[:, :, :].rearrange("p j e -> p (j e)"), scalar=TOP_K - 0.5,
                                               in1=rex[:, :, :].rearrange("p j e -> p (j e)"), op0=ALU.is_lt,
                                               op1=ALU.mult).then_inc(route.sem, 1)
                dve.wait_ge(route.sem, route.at(m, 9))
                nc.vector.tensor_reduce(rsum[:, :], rsl[:, :, :], AX_X, ALU.add).then_inc(route.sem, 1)
                dve.wait_ge(route.sem, route.at(m, 10))
                nc.vector.reciprocal(rrec[:, :], rsum[:, :]).then_inc(route.sem, 1)
                dve.wait_ge(route.sem, route.at(m, 11))

            def combine(m, k):
                dve.wait_ge(dn_done.sem, dn_done.at(m, k + 1))
                for j in range(TILES):
                    if k == 0:
                        dve.wait_ge(bias_ok.sem, bias_ok.at(m, 1))
                    else:
                        dve.wait_ge(acc_ok.sem, acc_ok.at(m, TILES * (k - 1) + j + 1))
                    nc.vector.scalar_tensor_tensor(out=yacc[:, j, :], in0=bank_b(j), scalar=comb[:, j, k:k + 1],
                                                   in1=yacc[:, j, :], op0=ALU.mult, op1=ALU.add).then_inc(acc_ok.sem, 1)

            def run(g, e, s, m):
                if g is not None:
                    for j in range(TILES):
                        dve.wait_ge(x_in[j].sem, x_in[j].at(g, 16))
                        stats(xg, st1, mv1, st1_ok, mv1_ok, g, j)
                if m is not None:
                    dve.wait_ge(o_ps.sem, o_ps.at(m, 1))
                    for j in range(TILES):
                        nc.vector.tensor_tensor(go[:, j, :], bank_b(j), mod[:, 2, :], ALU.mult).then_inc(go_ok.sem, 1)
                steps(s, 0, 2)
                if m is not None:
                    for j in range(TILES):
                        dve.wait_ge(xn_ok.sem, xn_ok.at(m, j + 1))
                        stats(xn, st2, mv2, st2_ok, mv2_ok, m, j)
                if g is not None:
                    for j in range(TILES):
                        normalise(xh, xg, mv1, rs1, rs1_ok, xh_ok, g, j)
                steps(s, 2, 4)
                if m is not None:
                    for j in range(TILES):
                        normalise(xh2, xn, mv2, rs2, rs2_ok, xh2_ok, m, j)
                if e is not None:
                    row_sum(e, 0)
                    row_inverse(e, 0)
                steps(s, 4, 8)
                if e is not None:
                    row_sum(e, 1)
                    row_inverse(e, 1)
                if m is not None:
                    routing(m)
                    nc.vector.tensor_tensor(comb[:, :, :], rsl[:, :, :], rrec[:, :].unsqueeze(2).broadcast_to([P, TILES, E]),
                                            ALU.mult).then_inc(comb_ok.sem, 1)
                for k in range(E):
                    steps(s, 8 + 3 * k, 11 + 3 * k)
                    if m is not None:
                        dve.wait_ge(sg_ok.sem, sg_ok.at(m, k + 1))
                        dve.wait_ge(clamp_ok.sem, clamp_ok.at(m, k + 1))
                        if k >= 2:
                            dve.wait_ge(dn_done.sem, dn_done.at(m, k - 1))
                        elif not is_first(m):
                            dve.wait_ge(dn_done.sem, dn_done.at(m - 1, E + k - 1))
                        nc.vector.scalar_tensor_tensor(out=act_t[:, k % 2, :], in0=sg[:, k % 2, :], scalar=SILU_LIMIT,
                                                       in1=up[:, k % 2, :], op0=ALU.min, op1=ALU.mult
                                                       ).then_inc(act_ok.sem, 1)
                        if k >= 1:
                            if k == 1:
                                dve.wait_ge(comb_ok.sem, comb_ok.at(m, 1))
                            combine(m, k - 1)
                    if g is not None and k in (3, 6):
                        row_max(g, (k - 3) // 3)
                if m is not None:
                    combine(m, E - 1)

            for lo, hi in whole(run):
                with dve.Fori(lo, hi) as it:
                    run(it, it - 1, it - 2, it - 3)

        @block.tensor
        def _(pe):
            pe.wait_ge(consts, CONSTS)
            pe.wait_ge(c_step, 4)
            nc.tensor.transpose(ps[:, 5, 0:B], c_rows[:, :], ident[0:B, 0:B]).then_inc(c_t, 1)
            pe.wait_ge(c_step, 5)
            pe.wait_ge(in_wmod, 16)
            nc.tensor.matmul(ps[:, 6, :], c_tok[:, :], wmod_sb[:, 0:512], start=True, stop=True).then_inc(mod_ps, 1)
            nc.tensor.matmul(ps[:, 7, 0:6 * D - 512], c_tok[:, :], wmod_sb[:, 512:6 * D], start=True,
                             stop=True).then_inc(mod_ps, 1)
            for n in range(N_GROUPS):
                bank = n % 6
                if n >= 6:
                    if n % 2 == 0:
                        pe.wait_ge(w_ev_act, (n - 6) // 2 + 1)
                    else:
                        pe.wait_ge(w_ev_dve, (n - 6) // 2 + 1)
                if n == 0:
                    pe.wait_ge(in_wa, 16)
                    pe.wait_ge(in_small, 16 * 6)
                    nc.tensor.transpose(ps[:, 0, 0:P], wa_rows[:, 0, :], ident[:, :])
                    nc.tensor.transpose(ps[:, 0, P:2 * P], wv_rows[:, :], ident[:, :])
                    nc.tensor.transpose(ps[:, 0, 2 * P:3 * P], wo_rows[:, :], ident[:, :])
                    last = nc.tensor.transpose(ps[:, 0, 3 * P:3 * P + E], rw_rows[:, :], ident[0:E, 0:E])
                elif n < N_WA:
                    for q in range(4):
                        last = nc.tensor.transpose(ps[:, bank, q * P:(q + 1) * P],
                                                   wa_rows[:, WA_GROUPS[n - 1][0] + q, :], ident[:, :])
                elif n < N_WA + E:
                    if n == N_WA:
                        pe.wait_ge(in_gu, 16)
                    for q in range(2 * KI):
                        last = nc.tensor.transpose(ps[:, bank, q * P:(q + 1) * P],
                                                   gu_rows[:, 2 * KI * (n - N_WA) + q, :], ident[:, :])
                elif n < N_GROUPS - 1:
                    if n == N_WA + E:
                        pe.wait_ge(in_dn, 16)
                    for q in range(4):
                        ee = (4 * (n - N_WA - E) + q) // KI
                        last = nc.tensor.transpose(ps[:, bank, q * P:(q + 1) * P],
                                                   dn_rows[:, ee, (q % KI) * P:(q % KI + 1) * P], ident[:, :])
                else:
                    last = nc.tensor.transpose(ps[:, bank, 0:E * 2 * KI], gub_rows[:, :],
                                               ident[0:E * 2 * KI, 0:E * 2 * KI])
                last.then_inc(w_ps, 1)
            pe.wait_ge(w_ev_act, (N_GROUPS + 1) // 2)
            pe.wait_ge(w_ev_dve, N_GROUPS // 2)
            pe.wait_ge(mod_ready, 1)

            def logits(g, n):
                j, k = n // KL, n % KL
                if n == 0:
                    pe.wait_ge(ht_ok.sem, ht_ok.at(g, 1))
                if n >= 2:
                    pe.wait_ge(lg_ev.sem, lg_ev.at(g, n - 1))
                elif not is_first(g):
                    pe.wait_ge(lg_ev.sem, lg_ev.at(g - 1, TILES * KL + n - 1))
                w = min(LC, NL - k * LC)
                nc.tensor.matmul(ps[:, n % 2, 0:w], ht[:, j * P:(j + 1) * P], wl[:, k * LC:k * LC + w], start=True,
                                 stop=True).then_inc(lg_ps.sem, 1)

            def gate_up(m, k):
                if k >= 2:
                    pe.wait_ge(up_ok.sem, up_ok.at(m, k - 1))
                elif not is_first(m):
                    pe.wait_ge(up_ok.sem, up_ok.at(m - 1, E + k - 1))
                for which in range(2):
                    for q in range(KI):
                        last = nc.tensor.matmul(gu_ps(k, which)[:, q * N:(q + 1) * N],
                                                wgu[:, k, which * I + q * P:which * I + (q + 1) * P], h2t[:, :],
                                                start=True, stop=True)
                    last.then_inc(gu_done.sem, 1)

            def down(m, k):
                pe.wait_ge(act_ok.sem, act_ok.at(m, k + 1))
                if k == 0:
                    pe.wait_ge(bias_ok.sem, bias_ok.at(m, 1))
                else:
                    pe.wait_ge(acc_ok.sem, acc_ok.at(m, TILES * k))
                for j in range(TILES):
                    for q in range(KI):
                        last = nc.tensor.matmul(bank_b(j), act_t[:, k % 2, q * N + j * P:q * N + (j + 1) * P],
                                                wd[:, k, q, :], start=(q == 0), stop=(q == KI - 1))
                last.then_inc(dn_done.sem, 1)

            def run(g, e, s, m):
                if m is not None:
                    if not is_first(m):
                        pe.wait_ge(combt_ok.sem, combt_ok.at(m - 1, 1))
                    else:
                        pe.wait_ge(ht_ok.sem, ht_ok.at(g - 1, 1))
                    for j in range(TILES):
                        pe.wait_ge(y_ld[j].sem, y_ld[j].at(m, 16 * B))
                        last = nc.tensor.transpose(bank_a(j), yt_tok[:, j, :], ident[:, :])
                    last.then_inc(yt_ps.sem, 1)
                    pe.wait_ge(yt_ok.sem, yt_ok.at(m, 1))
                    if not is_first(m):
                        pe.wait_ge(acc_ok.sem, acc_ok.at(m - 1, TILES * E))
                    for j in range(TILES):
                        last = nc.tensor.matmul(bank_b(j), yt[:, j * P:(j + 1) * P], wo[:, :], start=True, stop=True)
                    last.then_inc(o_ps.sem, 1)
                if g is not None:
                    if m is None and not is_first(g):
                        pe.wait_ge(ht_ok.sem, ht_ok.at(g - 1, 1))
                    pe.wait_ge(h_ok.sem, h_ok.at(g, TILES))
                    for j in range(TILES):
                        last = nc.tensor.transpose(bank_a(j), hh[:, j, :], ident[:, :])
                    last.then_inc(ht_ps.sem, 1)
                if m is not None:
                    pe.wait_ge(go_ok.sem, go_ok.at(m, TILES))
                    pe.wait_ge(h2_ok.sem, h2_ok.at(m, TILES))
                    for j in range(TILES):
                        last = nc.tensor.transpose(bank_b(j), h2[:, j, :], ident[:, :])
                    last.then_inc(h2t_ps.sem, 1)
                if g is not None:
                    logits(g, 0)
                    logits(g, 1)
                if m is not None:
                    if g is not None:
                        pe.wait_ge(ht_ok.sem, ht_ok.at(g, 1))
                    pe.wait_ge(h2t_ok.sem, h2t_ok.at(m, 1))
                    for j in range(TILES):
                        last = nc.tensor.matmul(bank_a(j)[:, 0:E], h2t[:, j * P:(j + 1) * P], rw[:, :], start=True,
                                                stop=True)
                    last.then_inc(r_ps.sem, 1)
                if g is not None:
                    for n in range(2, KL):
                        logits(g, n)
                for k in range(E):
                    if m is not None:
                        gate_up(m, k)
                        if k == 0:
                            pe.wait_ge(comb_ok.sem, comb_ok.at(m, 1))
                            for j in range(TILES):
                                last = nc.tensor.transpose(bank_a(j)[0:E, :], comb[:, j, :], ident[:, :])
                            last.then_inc(combt_ps.sem, 1)
                            pe.wait_ge(combt_ok.sem, combt_ok.at(m, 1))
                            for j in range(TILES):
                                last = nc.tensor.matmul(bank_b(j), combt[:, j * P:(j + 1) * P], bd[:, :], start=True,
                                                        stop=True)
                            last.then_inc(b_ps.sem, 1)
                        if k >= 1:
                            down(m, k - 1)
                    if g is not None and 1 <= k <= KL:
                        logits(g, KL + k - 1)
                if m is not None:
                    down(m, E - 1)

            for lo, hi in whole(run):
                with pe.Fori(lo, hi) as it:
                    run(it, it - 1, it - 2, it - 3)


_INS = ['L0_attn_x', 'L0_attn_norm_w', 'L0_attn_W_v', 'L0_attn_W_a', 'L0_attn_W_out', 'L0_ffn_router_weight',
        'L0_ffn_router_bias', 'L0_ffn_gate_up_proj', 'L0_ffn_gate_up_proj_bias', 'L0_ffn_down_proj',
        'L0_ffn_down_proj_bias', 'L0_c', 'L0_wmod']
_OUTS = [((8, 512, 128), 'float32')]


def kernel(**inputs):
    import numpy as _np
    import concourse.bacc as _bacc
    from concourse import mybir as _mybir
    from concourse.bass_utils import run_bass_kernel_spmd as _run

    nc = _bacc.Bacc("TRN2", target_bir_lowering=False, num_devices=1)
    arrays, args = {}, []
    for name in _INS:
        a = _np.ascontiguousarray(inputs[name])
        arrays[f"in_{name}_dram"] = a
        args.append(nc.dram_tensor(f"in_{name}_dram", a.shape, _mybir.dt.from_np(a.dtype), kind="ExternalInput").ap())
    for i, (shape, dtype) in enumerate(_OUTS):
        dt = _mybir.dt.from_np(_np.dtype(dtype))
        args.append(nc.dram_tensor(f"out_{i}_dram", shape, dt, kind="ExternalOutput").ap())
    adaln_block(nc, *args)
    r = _run(nc, [arrays], core_ids=[0])
    got = tuple(r.results[0][f"out_{i}_dram"] for i in range(len(_OUTS)))
    return got[0]
```

```python
from contextlib import ExitStack

import concourse.bass as bass
from concourse import mybir

F32 = mybir.dt.float32
ALU = mybir.AluOpType
ACT = mybir.ActivationFunctionType
AX_X = mybir.AxisListType.X

P = 128
EPS = 1e-5
ALPHA = 1.702
LIMIT = 7.0
TOP_K = 4
FLOOR = 0.25
SILU_LIMIT = 11.914 / (1.0 + 2.718281828459045 ** -11.914)


class Event:

    def __init__(self, sem, per):
        self.sem, self.per = sem, per

    def at(self, c, n):
        return c * self.per + n


def is_first(c):
    return isinstance(c, int) and c == 0


def adaln_block(nc, x, norm_w, w_v, w_a, w_out, router_w, router_b, gu_w, gu_b, down_w, down_b, cond, w_mod, out):
    B, T, D = x.shape
    E, I2, _ = gu_w.shape
    I = I2 // 2
    KI = I // P
    HI = D
    M = w_a.shape[0] // D - 1
    H = D // M
    M1 = M + 1
    NG = HI * M1
    NL = NG + D
    TS = P // B
    TILES = 2
    CS = TILES * TS
    NC = T // CS
    N = TILES * P
    HALF = M // 2
    ROW = HALF * M1
    BH = B * H
    LC = 512
    KL = -(-NL // LC)
    STEP_INCS = 4
    CONSTS = 9

    x_t = x.rearrange("b (n t) d -> n b t d", t=TS)
    out_t = out.rearrange("b (n t) d -> n b t d", t=TS)
    gate_dram = nc.dram_tensor("gate_dram", [TILES, B, H * 2, TS, ROW], F32, kind="Internal").ap()
    y_dram = nc.dram_tensor("y_dram", [TILES, B, H, TS, M], F32, kind="Internal").ap()

    with ExitStack() as ctx:
        def sb(name, shape):
            return ctx.enter_context(nc.sbuf_tensor(name, shape, F32))

        def sem(name):
            return ctx.enter_context(nc.semaphore(name))

        def event(name, per):
            return Event(sem(name), per)

        wa_rows = sb("wa_rows", [P, M1, D])
        gu_rows = sb("gu_rows", [P, E * 2 * KI, D])
        dn_rows = sb("dn_rows", [P, E, I])
        wv_rows = sb("wv_rows", [P, D])
        wo_rows = sb("wo_rows", [P, D])
        rw_rows = sb("rw_rows", [E, D])
        gub_rows = sb("gub_rows", [E * 2 * KI, P])
        c_rows = sb("c_rows", [B, D])
        c_tmp = sb("c_tmp", [B, 3, D])
        c_col = sb("c_col", [P, B])
        c_tok = sb("c_tok", [P, P])
        wmod_sb = sb("wmod_sb", [P, 6 * D])
        nw = sb("nw", [P, 1])
        nws = sb("nws", [P, 1])
        wl = sb("wl", [P, NL])
        wgu = sb("wgu", [P, E, I2])
        wd = sb("wd", [P, E, KI, D])
        wo = sb("wo", [P, D])
        rw = sb("rw", [P, E])
        bgu = sb("bgu", [P, E, 2 * KI])
        bd = sb("bd", [E, D])
        rb = sb("rb", [P, E])
        mod = sb("mod", [P, 6, D])
        g_abs = sb("g_abs", [P, D])
        ident = sb("ident", [P, P])
        lower = sb("lower", [P, E, E])
        minus_half = sb("minus_half", [P, 1])
        eps_mean = sb("eps_mean", [P, 1])
        eps_sum = sb("eps_sum", [P, 1])
        xg = sb("xg", [P, TILES, D])
        st1 = sb("st1", [P, TILES, 6])
        mv1 = sb("mv1", [P, TILES, 2])
        ve1 = sb("ve1", [P, TILES, 1])
        rs1 = sb("rs1", [P, TILES, 1])
        xh = sb("xh", [P, TILES, D])
        hh = sb("hh", [P, TILES, D])
        res = sb("res", [P, TILES, D])
        sq_junk = sb("sq_junk", [P, TILES, D])
        ms = sb("ms", [P, TILES, 1])
        me = sb("me", [P, TILES, 1])
        rms = sb("rms", [P, TILES, 1])
        ht = sb("ht", [P, N])
        lg = sb("lg", [P, TILES, NG])
        vv = sb("vv", [P, TILES, HI])
        nmax = sb("nmax", [P, TILES, HI])
        ex = sb("ex", [P, TILES, NG])
        zs = sb("zs", [P, TILES, HI])
        rz = sb("rz", [P, TILES, HI])
        rv = sb("rv", [P, TILES, HI])
        gates = sb("gates", [P, CS, ROW])
        state = sb("state", [P, CS, M1])
        prod = sb("prod", [P, ROW])
        yt_tok = sb("yt_tok", [P, TILES, HI])
        yt = sb("yt", [P, N])
        r_in = sb("r_in", [P, TILES, D])
        go = sb("go", [P, TILES, D])
        xn = sb("xn", [P, TILES, D])
        st2 = sb("st2", [P, TILES, 6])
        mv2 = sb("mv2", [P, TILES, 2])
        ve2 = sb("ve2", [P, TILES, 1])
        rs2 = sb("rs2", [P, TILES, 1])
        xm = sb("xm", [P, TILES, D])
        xh2 = sb("xh2", [P, TILES, D])
        h2 = sb("h2", [P, TILES, D])
        h2t_next = sb("h2t_next", [P, N])
        h2t = sb("h2t", [P, N])
        rl = sb("rl", [P, TILES, E])
        rmx = sb("rmx", [P, TILES])
        rgt = sb("rgt", [P, TILES, E, E])
        req = sb("req", [P, TILES, E, E])
        rank = sb("rank", [P, TILES, E])
        chosen = sb("chosen", [P, TILES, E])
        rdl = sb("rdl", [P, TILES, E])
        rex = sb("rex", [P, TILES, E])
        rsl = sb("rsl", [P, TILES, E])
        rsum = sb("rsum", [P, TILES])
        rrec = sb("rrec", [P, TILES])
        comb = sb("comb", [P, TILES, E])
        combt = sb("combt", [E, N])
        sg = sb("sg", [P, 2, KI * N])
        up = sb("up", [P, 2, KI * N])
        act_t = sb("act_t", [P, 2, KI * N])
        weighted = sb("weighted", [P, 2, TILES, D])
        yacc = sb("yacc", [P, TILES, D])
        gy = sb("gy", [P, TILES, D])
        res_out = sb("res_out", [P, TILES, D])

        ps = ctx.enter_context(nc.psum_tensor("ps", [P, 8, 512], F32))

        def gu_ps(e, which):
            return ps[:, 2 + 2 * (e % 2) + which, :]

        def bank_a(j):
            return ps[:, 6, j * P:(j + 1) * P]

        def dn_ps(j):
            return ps[:, 7, j * P:(j + 1) * P]

        in_c, in_wmod, in_nw, in_wa = sem("in_c"), sem("in_wmod"), sem("in_nw"), sem("in_wa")
        in_small, in_gu, in_dn = sem("in_small"), sem("in_gu"), sem("in_dn")
        consts = sem("consts")
        passed_sp, passed_pool, passed_dve = sem("passed_sp"), sem("passed_pool"), sem("passed_dve")
        c_step = sem("c_step")
        c_t, nws_ok = sem("c_t"), sem("nws_ok")
        mod_ps, mod_step = sem("mod_ps"), sem("mod_step")
        mod_ready = sem("mod_ready")
        w_ps, w_ev_act, w_ev_dve = sem("w_ps"), sem("w_ev_act"), sem("w_ev_dve")
        x_in = [event(f"x_in{j}", 16) for j in range(TILES)]
        st1_ok, mv1_ok = event("st1_ok", TILES), event("mv1_ok", TILES)
        ve1_ok, rs1_ok = event("ve1_ok", 1), event("rs1_ok", 1)
        xh_ok, hm_ok, h_ok = event("xh_ok", TILES), event("hm_ok", 1), event("h_ok", 1)
        gh_ok, res_ok = event("gh_ok", 1), event("res_ok", 1)
        res_st = [event(f"res_st{j}", 16) for j in range(TILES)]
        ms_ok, me_ok, rms_ok = event("ms_ok", TILES), event("me_ok", 1), event("rms_ok", 1)
        ht_ps, ht_ok = event("ht_ps", 1), event("ht_ok", 1)
        lg_ps, lg_ev = event("lg_ps", TILES * KL), event("lg_ev", TILES * KL)
        nmax_ok = event("nmax_ok", TILES * H)
        sub_ok = event("sub_ok", 2 * TILES)
        exp_ok = event("exp_ok", TILES)
        zs_ok, rz_ok, rv_ok = event("zs_ok", TILES * H), event("rz_ok", TILES), event("rv_ok", TILES)
        norm_ok = event("norm_ok", 2 * TILES)
        g_st = [event(f"g_st{j}", 16 * B) for j in range(TILES)]
        g_ld = [event(f"g_ld{j}", 32) for j in range(TILES)]
        scan = event("scan", STEP_INCS * CS)
        y_st = [event(f"y_st{j}", 16) for j in range(TILES)]
        y_ld = [event(f"y_ld{j}", 16 * B) for j in range(TILES)]
        yt_ps, yt_ok, o_ps = event("yt_ps", 1), event("yt_ok", 1), event("o_ps", 1)
        r_ld = [event(f"r_ld{j}", 16) for j in range(TILES)]
        go_ok, xn_ok = event("go_ok", TILES), event("xn_ok", 1)
        st2_ok, mv2_ok = event("st2_ok", TILES), event("mv2_ok", TILES)
        ve2_ok, rs2_ok = event("ve2_ok", 1), event("rs2_ok", 1)
        xh2_ok, hm2_ok, h2_ok = event("xh2_ok", TILES), event("hm2_ok", 1), event("h2_ok", 1)
        h2t_ps, h2t_next_ok = event("h2t_ps", 1), event("h2t_next_ok", 1)
        r_ps = event("r_ps", 1)
        rank_in = event("rank_in", 7)
        rex_ok = event("rex_ok", 1)
        xm_ld = event("xm_ld", 16)
        h2t_ok = event("h2t_ok", 1)
        weigh = event("weigh", 5)
        combt_ps, combt_ok, b_ps = event("combt_ps", 1), event("combt_ok", 1), event("b_ps", 1)
        bias_ok = event("bias_ok", 1)
        gu_done = event("gu_done", 2 * E)
        sg_ok, up_ok = event("sg_ok", E), event("up_ok", E)
        clamp_ok = event("clamp_ok", E)
        act_ok = event("act_ok", KI * E)
        dn_done = event("dn_done", E)
        weighted_ok, acc_ok = event("weighted_ok", E), event("acc_ok", E)
        gy_ok, ro_ok = event("gy_ok", 1), event("ro_ok", 1)
        out_st = [event(f"out_st{j}", 16) for j in range(TILES)]

        block = ctx.enter_context(nc.Block())

        DEPTH = 7

        def whole(eng, run):
            def peeled(it):
                run(*[it - d if 0 <= it - d < NC else None for d in range(DEPTH)])

            for it in range(DEPTH):
                peeled(it)
            with eng.Fori(DEPTH, NC) as it:
                run(*[it - d for d in range(DEPTH)])
            for it in range(NC, NC + DEPTH - 1):
                peeled(it)

        WA_GROUPS = [(1, 4), (5, 4), (9, 4), (13, 4)]
        N_WA = 1 + len(WA_GROUPS)
        N_GROUPS = N_WA + E + E * KI // 4 + 1

        def wl_dst(j0, n, half):
            if half == 0 or j0 == 0:
                to = j0
            else:
                to = (j0 - 1 + HALF) % M + 1
            v = wl[:, 0:NG].rearrange("p (h g i j) -> p j h g i", h=H, g=2, i=HALF)
            return v[:, to:to + n, :, half, :]

        def wl_src(bank, n, half):
            v = ps[:, bank, 0:n * P].rearrange("p (j h g i) -> p j h g i", j=n, h=H, g=2)
            return v[:, :, :, half, :]

        @block.sync
        def _(sp):
            sp.dma_start(c_rows[:, :], cond).then_inc(in_c, 16)
            sp.dma_start(wmod_sb[:, :], w_mod).then_inc(in_wmod, 16)
            sp.dma_start(nw[:, :], norm_w.rearrange("(d o) -> d o", o=1)).then_inc(in_nw, 16)
            sp.dma_start(wa_rows[:, :, :], w_a.rearrange("(r j) d -> r j d", j=M1)).then_inc(in_wa, 16)
            sp.dma_start(wv_rows[:, :], w_v).then_inc(in_small, 16)
            sp.dma_start(wo_rows[:, :], w_out).then_inc(in_small, 16)
            sp.dma_start(rw_rows[:, :], router_w).then_inc(in_small, 16)
            sp.dma_start(gub_rows[:, :], gu_b.rearrange("e (k p) -> (e k) p", p=P)).then_inc(in_small, 16)
            sp.dma_start(bd[:, :], down_b).then_inc(in_small, 16)
            sp.dma_start(rb[:, :], router_b.partition_broadcast(P)).then_inc(in_small, 16)

            def run(a, g, e, s, p, m, o):
                if a is not None:
                    if not is_first(a):
                        sp.wait_ge(res_ok.sem, res_ok.at(a - 1, 1))
                        sp.sem_inc(passed_sp, 1)
                    for j in range(TILES):
                        sp.dma_start(xg[:, j, :], x_t[2 * a + j]).then_inc(x_in[j].sem, 16)
                if p is not None:
                    for j in range(TILES):
                        sp.wait_ge(res_st[j].sem, res_st[j].at(p, 16))
                        sp.sem_inc(passed_sp, 1)
                    if not is_first(p):
                        sp.wait_ge(xn_ok.sem, xn_ok.at(p - 1, 1))
                        sp.sem_inc(passed_sp, 1)
                    for j in range(TILES):
                        sp.dma_start(r_in[:, j, :], out_t[2 * p + j]).then_inc(r_ld[j].sem, 16)
                if o is not None:
                    sp.wait_ge(ro_ok.sem, ro_ok.at(o, 1))
                    sp.sem_inc(passed_sp, 1)
                if m is not None:
                    sp.wait_ge(xn_ok.sem, xn_ok.at(m, 1))
                    sp.sem_inc(passed_sp, 1)
                    sp.dma_start(xm[:, :, :], xn[:, :, :]).then_inc(xm_ld.sem, 16)
                if o is not None:
                    for j in range(TILES):
                        sp.dma_start(out_t[2 * o + j], res_out[:, j, :]).then_inc(out_st[j].sem, 16)
                if isinstance(a, int) and a == 0:
                    sp.dma_start(gu_rows[:, :, :], gu_w.rearrange("e (k p) d -> p (e k) d", p=P)).then_inc(in_gu, 16)
                    sp.dma_start(dn_rows[:, :, :], down_w.rearrange("e d i -> d e i")).then_inc(in_dn, 16)
                if e is not None:
                    for j in range(TILES):
                        sp.wait_ge(norm_ok.sem, norm_ok.at(e, 2 * j + 2))
                        sp.sem_inc(passed_sp, 1)
                        if not is_first(e):
                            sp.wait_ge(g_ld[j].sem, g_ld[j].at(e, 0))
                            sp.sem_inc(passed_sp, 1)
                        for b in range(B):
                            sp.dma_start(gate_dram[j, b].rearrange("r t e -> t r e"),
                                         ex[b * TS:(b + 1) * TS, j, :].rearrange("p (r e) -> p r e", e=ROW)
                                         ).then_inc(g_st[j].sem, 16)
                for j in range(TILES):
                    if j == TILES - 1 and a is not None:
                        sp.wait_ge(res_ok.sem, res_ok.at(a, 1))
                        sp.sem_inc(passed_sp, 1)
                        for i in range(TILES):
                            sp.dma_start(out_t[2 * a + i], res[:, i, :]).then_inc(res_st[i].sem, 16)
                    if s is not None:
                        sp.wait_ge(scan.sem, scan.at(s, STEP_INCS * TS * (j + 1)))
                        sp.sem_inc(passed_sp, 1)
                        if not is_first(s):
                            sp.wait_ge(y_ld[j].sem, y_ld[j].at(s, 0))
                            sp.sem_inc(passed_sp, 1)
                        sp.dma_start(y_dram[j].rearrange("b h t i -> (b h) t i"),
                                     state[0:BH, j * TS:(j + 1) * TS, 1:M1]).then_inc(y_st[j].sem, 16)
                    if e is not None:
                        sp.wait_ge(g_st[j].sem, g_st[j].at(e, 16 * B))
                        sp.sem_inc(passed_sp, 1)
                        for half in range(2):
                            sp.dma_start(gates[half * BH:(half + 1) * BH, j * TS:(j + 1) * TS, :],
                                         gate_dram[j].rearrange("b (h g) t e -> g (b h) t e", g=2)[half]
                                         ).then_inc(g_ld[j].sem, 16)
                    if s is not None:
                        sp.wait_ge(y_st[j].sem, y_st[j].at(s, 16))
                        sp.sem_inc(passed_sp, 1)
                        if not is_first(s):
                            sp.wait_ge(yt_ps.sem, yt_ps.at(s - 1, 1))
                            sp.sem_inc(passed_sp, 1)
                        for b in range(B):
                            sp.dma_start(yt_tok[b * TS:(b + 1) * TS, j, :].rearrange("t (h i) -> t h i", h=H),
                                         y_dram[j, b].rearrange("h t i -> t h i")).then_inc(y_ld[j].sem, 16)

            whole(sp, run)
            for j in range(TILES):
                sp.wait_ge(out_st[j].sem, out_st[j].at(NC, 0))

        @block.gpsimd
        def _(pool):
            nc.gpsimd.memset(ident[:, :], 0.0).then_inc(consts, 1)
            nc.gpsimd.memset(lower[:, :, :], 1.0).then_inc(consts, 1)
            nc.gpsimd.memset(minus_half[:, :], -0.5).then_inc(consts, 1)
            nc.gpsimd.memset(eps_mean[:, :], EPS).then_inc(consts, 1)
            nc.gpsimd.memset(eps_sum[:, :], EPS * D).then_inc(consts, 1)
            nc.gpsimd.memset(state[:, :, :], 0.0).then_inc(consts, 1)
            pool.wait_ge(consts, 6)
            nc.gpsimd.memset(state[:, :, 0:1], 1.0).then_inc(consts, 1)
            nc.gpsimd.affine_select(out=ident[:, :], in_=ident[:, :], compare_op=ALU.not_equal, fill=1.0, base=0,
                                    pattern=[[-1, P]], channel_multiplier=1).then_inc(consts, 1)
            nc.gpsimd.affine_select(out=lower[:, :, :], in_=lower[:, :, :], compare_op=ALU.is_gt, fill=0.0, base=0,
                                    pattern=[[1, E], [-1, E]], channel_multiplier=0).then_inc(consts, 1)

            def both(row):
                return mod[:, row, :].unsqueeze(1).broadcast_to([P, TILES, D])

            def inv_sqrt(src, eps, mid, dst, mid_ok, dst_ok, c):
                nc.gpsimd.tensor_tensor(mid[:, :, 0], src, eps[:, :].broadcast_to([P, TILES]), ALU.add
                                        ).then_inc(mid_ok.sem, 1)
                pool.wait_ge(mid_ok.sem, mid_ok.at(c, 1))
                nc.gpsimd.tensor_tensor(dst[:, :, 0], mid[:, :, 0], minus_half[:, :].broadcast_to([P, TILES]), ALU.pow
                                        ).then_inc(dst_ok.sem, 1)

            def norm_gates(e, j, part):
                if part == 0:
                    pool.wait_ge(rv_ok.sem, rv_ok.at(e, j + 1))
                lo, hi = part * HI // 2, (part + 1) * HI // 2
                v = ex[:, j, :].rearrange("p (r k) -> p r k", k=M1)[:, lo:hi, :]
                nc.gpsimd.tensor_tensor(v[:, :, 0], v[:, :, 0], rv[:, j, lo:hi], ALU.mult)
                nc.gpsimd.tensor_tensor(v[:, :, 1:M1], v[:, :, 1:M1],
                                        rz[:, j, lo:hi].unsqueeze(2).broadcast_to([P, HI // 2, M]),
                                        ALU.mult).then_inc(norm_ok.sem, 1)

            def sub_max(g, j, part):
                lo, hi = part * HI // 2, (part + 1) * HI // 2
                pool.wait_ge(nmax_ok.sem, nmax_ok.at(g, H * j + H // 2 * (part + 1)))
                v = lg[:, j, :].rearrange("p (r k) -> p r k", k=M1)[:, lo:hi, :]
                nc.gpsimd.tensor_tensor(v, v, nmax[:, j, lo:hi].unsqueeze(2).broadcast_to([P, HI // 2, M1]),
                                        ALU.add).then_inc(sub_ok.sem, 1)

            def first_h(a):
                if is_first(a):
                    pool.wait_ge(mod_ready, 1)
                else:
                    pool.wait_ge(ht_ps.sem, ht_ps.at(a - 1, 1))
                pool.wait_ge(xh_ok.sem, xh_ok.at(a, TILES))
                nc.gpsimd.tensor_tensor(hh[:, :, :], xh[:, :, :], both(1), ALU.mult).then_inc(hm_ok.sem, 1)
                pool.wait_ge(hm_ok.sem, hm_ok.at(a, 1))
                nc.gpsimd.tensor_tensor(hh[:, :, :], hh[:, :, :], both(0), ALU.add).then_inc(h_ok.sem, 1)

            def residual(a):
                if not is_first(a):
                    for j in range(TILES):
                        pool.wait_ge(res_st[j].sem, res_st[j].at(a, 0))
                nc.gpsimd.tensor_tensor(res[:, :, :], hh[:, :, :], both(2), ALU.mult).then_inc(gh_ok.sem, 1)
                pool.wait_ge(gh_ok.sem, gh_ok.at(a, 1))
                nc.gpsimd.tensor_tensor(res[:, :, :], res[:, :, :], xg[:, :, :], ALU.add).then_inc(res_ok.sem, 1)

            def new_residual(p):
                pool.wait_ge(go_ok.sem, go_ok.at(p, TILES))
                if not is_first(p):
                    pool.wait_ge(xm_ld.sem, xm_ld.at(p, 0))
                for j in range(TILES):
                    pool.wait_ge(r_ld[j].sem, r_ld[j].at(p, 16))
                nc.gpsimd.tensor_tensor(xn[:, :, :], go[:, :, :], r_in[:, :, :], ALU.add).then_inc(xn_ok.sem, 1)

            def second_h(p):
                pool.wait_ge(xh2_ok.sem, xh2_ok.at(p, TILES))
                nc.gpsimd.tensor_tensor(h2[:, :, :], xh2[:, :, :], both(4), ALU.mult).then_inc(hm2_ok.sem, 1)
                pool.wait_ge(hm2_ok.sem, hm2_ok.at(p, 1))
                nc.gpsimd.tensor_tensor(h2[:, :, :], h2[:, :, :], both(3), ALU.add).then_inc(h2_ok.sem, 1)

            def accumulate(m, k):
                pool.wait_ge(weighted_ok.sem, weighted_ok.at(m, k + 1))
                if k == 0:
                    pool.wait_ge(bias_ok.sem, bias_ok.at(m, 1))
                else:
                    pool.wait_ge(acc_ok.sem, acc_ok.at(m, k))
                nc.gpsimd.tensor_tensor(yacc[:, :, :], yacc[:, :, :], weighted[:, k % 2, :, :], ALU.add
                                        ).then_inc(acc_ok.sem, 1)

            def run(a, g, e, s, p, m, o):
                for k in range(E):
                    if m is not None and k >= 1:
                        accumulate(m, k - 1)
                    if k == 2 and a is not None:
                        pool.wait_ge(mv1_ok.sem, mv1_ok.at(a, TILES))
                        inv_sqrt(mv1[:, :, 1], eps_mean, ve1, rs1, ve1_ok, rs1_ok, a)
                    if e is not None:
                        if k == 2:
                            norm_gates(e, 0, 0)
                            norm_gates(e, 0, 1)
                        if k == 4:
                            norm_gates(e, 1, 0)
                            norm_gates(e, 1, 1)
                    if k == 3 and a is not None:
                        first_h(a)
                    if k == 4 and p is not None:
                        new_residual(p)
                    if k == 5:
                        if p is not None:
                            pool.wait_ge(mv2_ok.sem, mv2_ok.at(p, TILES))
                            inv_sqrt(mv2[:, :, 1], eps_mean, ve2, rs2, ve2_ok, rs2_ok, p)
                        if a is not None:
                            pool.wait_ge(ms_ok.sem, ms_ok.at(a, TILES))
                            if g is not None:
                                pool.wait_ge(lg_ev.sem, lg_ev.at(g, TILES * KL))
                            inv_sqrt(ms[:, :, 0], eps_sum, me, rms, me_ok, rms_ok, a)
                        if g is not None:
                            sub_max(g, 0, 0)
                    if k == 6:
                        if p is not None:
                            second_h(p)
                        if g is not None:
                            sub_max(g, 0, 1)
                        if a is not None:
                            residual(a)
                    if k == 7 and g is not None:
                        sub_max(g, 1, 0)
                if g is not None:
                    sub_max(g, 1, 1)
                if m is not None:
                    accumulate(m, E - 1)
                    pool.wait_ge(acc_ok.sem, acc_ok.at(m, E))
                    nc.gpsimd.tensor_tensor(gy[:, :, :], yacc[:, :, :], both(5), ALU.mult).then_inc(gy_ok.sem, 1)
                    if not is_first(m):
                        for j in range(TILES):
                            pool.wait_ge(out_st[j].sem, out_st[j].at(m, 0))
                    pool.wait_ge(xm_ld.sem, xm_ld.at(m, 16))
                    pool.wait_ge(gy_ok.sem, gy_ok.at(m, 1))
                    nc.gpsimd.tensor_tensor(res_out[:, :, :], gy[:, :, :], xm[:, :, :], ALU.add).then_inc(ro_ok.sem, 1)

            whole(pool, run)

        @block.scalar
        def _(act):
            act.wait_ge(in_c, 16)
            nc.scalar.activation(c_tmp[:, 0, :], c_rows[:, :], ACT.Exp, scale=-1.0).then_inc(c_step, 1)
            for k in range(6):
                act.wait_ge(mod_ps, 2)
                src = ps[:, 6 + k // 4, (k % 4) * P:(k % 4 + 1) * P]
                if k in (1, 4):
                    nc.scalar.activation(mod[:, k, :], src, ACT.Copy, bias=1.0).then_inc(mod_step, 1)
                else:
                    nc.scalar.activation(mod[:, k, :], src, ACT.Copy).then_inc(mod_step, 1)
            act.wait_ge(nws_ok, 1)
            act.wait_ge(w_ps, 1)
            for half in range(2):
                nc.scalar.activation(wl_dst(0, 1, half), wl_src(0, 1, half), ACT.Copy, scale=nws[:, 0:1])
            nc.scalar.activation(wl[:, NG:NL], ps[:, 0, P:2 * P], ACT.Copy, scale=nws[:, 0:1])
            nc.scalar.activation(wo[:, :], ps[:, 0, 2 * P:3 * P], ACT.Copy)
            nc.scalar.activation(rw[:, :], ps[:, 0, 3 * P:3 * P + E], ACT.Copy).then_inc(w_ev_act, 1)
            for n in range(1, N_GROUPS):
                if n % 2:
                    continue
                act.wait_ge(w_ps, n + 1)
                bank = n % 6
                if n < N_WA:
                    for half in range(2):
                        last = nc.scalar.activation(wl_dst(*WA_GROUPS[n - 1], half), wl_src(bank, 4, half), ACT.Copy,
                                                    scale=nws[:, 0:1])
                elif n < N_WA + E:
                    last = nc.scalar.activation(wgu[:, n - N_WA, :], ps[:, bank, :], ACT.Copy)
                elif n < N_GROUPS - 1:
                    q = n - N_WA - E
                    last = nc.scalar.activation(wd[:, 2 * q:2 * q + 2, :, :], ps[:, bank, :], ACT.Copy, scale=1.0 / ALPHA)
                else:
                    v = ps[:, bank, 0:E * 2 * KI].rearrange("p (e k) -> p e k", e=E)
                    nc.scalar.activation(bgu[:, :, 0:KI], v[:, :, 0:KI], ACT.Copy, scale=ALPHA)
                    last = nc.scalar.activation(bgu[:, :, KI:2 * KI], v[:, :, KI:2 * KI], ACT.Copy, bias=1.0)
                last.then_inc(w_ev_act, 1)

            def softmax_exp(e, j):
                act.wait_ge(sub_ok.sem, sub_ok.at(e, 2 * j + 2))
                if not is_first(e):
                    act.wait_ge(g_st[j].sem, g_st[j].at(e, 0))
                nc.scalar.activation(ex[:, j, :], lg[:, j, :], ACT.Exp).then_inc(exp_ok.sem, 1)

            def logits_out(g, n):
                j, k = n // KL, n % KL
                if k == 0:
                    act.wait_ge(rms_ok.sem, rms_ok.at(g, 1))
                    if not is_first(g):
                        act.wait_ge(exp_ok.sem, exp_ok.at(g - 1, j + 1))
                act.wait_ge(lg_ps.sem, lg_ps.at(g, n + 1))
                bank = n % 2
                if k < KL - 1:
                    nc.scalar.activation(lg[:, j, k * LC:(k + 1) * LC], ps[:, bank, :], ACT.Copy,
                                         scale=rms[:, j, :]).then_inc(lg_ev.sem, 1)
                else:
                    w = NG - k * LC
                    nc.scalar.activation(lg[:, j, k * LC:NG], ps[:, bank, 0:w], ACT.Copy, scale=rms[:, j, :])
                    if not is_first(g):
                        act.wait_ge(rv_ok.sem, rv_ok.at(g - 1, j + 1))
                    nc.scalar.activation(vv[:, j, :], ps[:, bank, w:w + D], ACT.Copy,
                                         scale=rms[:, j, :]).then_inc(lg_ev.sem, 1)

            def silu_and_up(m, k):
                act.wait_ge(gu_done.sem, gu_done.at(m, 2 * k + 1))
                if k >= 2:
                    act.wait_ge(act_ok.sem, act_ok.at(m, KI * (k - 1)))
                elif not is_first(m):
                    act.wait_ge(act_ok.sem, act_ok.at(m - 1, KI * (E + k - 1)))
                for q in range(KI):
                    last = nc.scalar.activation(sg[:, k % 2, q * N:(q + 1) * N], gu_ps(k, 0)[:, q * N:(q + 1) * N],
                                                ACT.Silu, bias=bgu[:, k, q:q + 1], scale=ALPHA)
                last.then_inc(sg_ok.sem, 1)
                act.wait_ge(gu_done.sem, gu_done.at(m, 2 * k + 2))
                for q in range(KI):
                    last = nc.scalar.activation(up[:, k % 2, q * N:(q + 1) * N], gu_ps(k, 1)[:, q * N:(q + 1) * N],
                                                ACT.Identity, bias=bgu[:, k, KI + q:KI + q + 1])
                last.then_inc(up_ok.sem, 1)

            def weigh_expert(m, k):
                act.wait_ge(dn_done.sem, dn_done.at(m, k + 1))
                act.wait_ge(weigh.sem, weigh.at(m, 5))
                if k >= 2:
                    act.wait_ge(acc_ok.sem, acc_ok.at(m, k - 1))
                elif not is_first(m):
                    act.wait_ge(acc_ok.sem, acc_ok.at(m - 1, E + k - 1))
                for j in range(TILES):
                    last = nc.scalar.activation(weighted[:, k % 2, j, :], dn_ps(j), ACT.Copy, scale=comb[:, j, k:k + 1])
                last.then_inc(weighted_ok.sem, 1)

            def run(a, g, e, s, p, m, o):
                if e is not None:
                    for j in range(TILES):
                        softmax_exp(e, j)
                for k in range(E):
                    if m is not None:
                        silu_and_up(m, k)
                        if k == 1:
                            act.wait_ge(combt_ps.sem, combt_ps.at(m, 1))
                            nc.scalar.activation(combt[:, :], ps[0:E, 6, 0:N], ACT.Copy).then_inc(combt_ok.sem, 1)
                    if g is not None and k < KL:
                        logits_out(g, 2 * k)
                    if m is not None:
                        if k == 1:
                            act.wait_ge(b_ps.sem, b_ps.at(m, 1))
                            if not is_first(m):
                                act.wait_ge(gy_ok.sem, gy_ok.at(m - 1, 1))
                            nc.scalar.activation(yacc[:, :, :].rearrange("p j d -> p (j d)"), ps[:, 6, 0:N],
                                                 ACT.Copy).then_inc(bias_ok.sem, 1)
                        if k >= 1:
                            weigh_expert(m, k - 1)
                    if g is not None and k < KL:
                        logits_out(g, 2 * k + 1)
                    if k == 2 and p is not None:
                        act.wait_ge(yt_ps.sem, yt_ps.at(p, 1))
                        nc.scalar.activation(yt[:, :], ps[:, 6, 0:N], ACT.Copy).then_inc(yt_ok.sem, 1)
                    if k == 3 and a is not None:
                        act.wait_ge(h_ok.sem, h_ok.at(a, 1))
                        for j in range(TILES):
                            nc.scalar.activation(sq_junk[:, j, :], hh[:, j, :], ACT.Square,
                                                 accum_out=ms[:, j, :]).then_inc(ms_ok.sem, 1)
                    if k == 5 and a is not None:
                        act.wait_ge(ht_ps.sem, ht_ps.at(a, 1))
                        nc.scalar.activation(ht[:, :], ps[:, 6, 0:N], ACT.Copy).then_inc(ht_ok.sem, 1)
                    if k == 6 and p is not None:
                        act.wait_ge(h2t_ps.sem, h2t_ps.at(p, 1))
                        if m is not None:
                            act.wait_ge(h2t_ok.sem, h2t_ok.at(m, 1))
                        nc.scalar.activation(h2t_next[:, :], ps[:, 6, 0:N], ACT.Copy).then_inc(h2t_next_ok.sem, 1)
                if m is not None:
                    weigh_expert(m, E - 1)
                if p is not None:
                    act.wait_ge(rank_in.sem, rank_in.at(p, 7))
                    nc.scalar.activation(rex[:, :, :], rdl[:, :, :], ACT.Exp).then_inc(rex_ok.sem, 1)

            whole(act, run)

        @block.vector
        def _(dve):
            dve.wait_ge(c_step, 1)
            nc.vector.tensor_scalar(c_tmp[:, 1, :], c_tmp[:, 0, :], 1.0, None, ALU.add).then_inc(c_step, 1)
            dve.wait_ge(c_step, 2)
            nc.vector.reciprocal(c_tmp[:, 2, :], c_tmp[:, 1, :]).then_inc(c_step, 1)
            dve.wait_ge(c_step, 3)
            nc.vector.tensor_tensor(c_rows[:, :], c_rows[:, :], c_tmp[:, 2, :], ALU.mult).then_inc(c_step, 1)
            dve.wait_ge(c_t, 1)
            nc.vector.tensor_copy(c_tok[:, :].rearrange("p (b t) -> p b t", b=B),
                                  ps[:, 5, 0:B].unsqueeze(2).broadcast_to([P, B, TS])).then_inc(c_step, 1)
            done = 6
            for k in (2, 5):
                dve.wait_ge(mod_step, done)
                nc.vector.scalar_tensor_tensor(out=g_abs[:, :], in0=mod[:, k, :], scalar=-1.0, in1=mod[:, k, :],
                                               op0=ALU.mult, op1=ALU.max).then_inc(mod_step, 1)
                done += 1
                dve.wait_ge(mod_step, done)
                nc.vector.tensor_scalar(g_abs[:, :], g_abs[:, :], FLOOR, None, ALU.max).then_inc(mod_step, 1)
                nc.vector.tensor_scalar(mod[:, k, :], mod[:, k, :], 0.0, 2.0, ALU.is_ge, ALU.mult).then_inc(mod_step, 1)
                done += 2
                dve.wait_ge(mod_step, done)
                last = nc.vector.scalar_tensor_tensor(out=mod[:, k, :], in0=mod[:, k, :], scalar=-1.0, in1=g_abs[:, :],
                                                      op0=ALU.add, op1=ALU.mult)
                if k == 2:
                    last.then_inc(mod_step, 1)
                    done += 1
                else:
                    last.then_inc(mod_ready, 1)
            dve.wait_ge(in_nw, 16)
            nc.vector.tensor_scalar(nws[:, :], nw[:, :], float(D) ** 0.5, None, ALU.mult).then_inc(nws_ok, 1)
            dve.wait_ge(nws_ok, 1)
            for n in range(1, N_GROUPS):
                if n % 2 == 0:
                    continue
                dve.wait_ge(w_ps, n + 1)
                bank = n % 6
                if n < N_WA:
                    for half in range(2):
                        last = nc.vector.tensor_scalar(wl_dst(*WA_GROUPS[n - 1], half), wl_src(bank, 4, half),
                                                       nws[:, 0:1], None, ALU.mult)
                elif n < N_WA + E:
                    last = nc.vector.tensor_copy(wgu[:, n - N_WA, :], ps[:, bank, :])
                elif n < N_GROUPS - 1:
                    q = n - N_WA - E
                    last = nc.vector.tensor_scalar(wd[:, 2 * q:2 * q + 2, :, :].rearrange("p e k d -> p (e k d)"),
                                                   ps[:, bank, :], 1.0 / ALPHA, None, ALU.mult)
                else:
                    v = ps[:, bank, 0:E * 2 * KI].rearrange("p (e k) -> p e k", e=E)
                    nc.vector.tensor_scalar(bgu[:, :, 0:KI], v[:, :, 0:KI], ALPHA, None, ALU.mult)
                    last = nc.vector.tensor_scalar(bgu[:, :, KI:2 * KI], v[:, :, KI:2 * KI], 1.0, None, ALU.add)
                last.then_inc(w_ev_dve, 1)
            dve.wait_ge(consts, CONSTS)

            def normalise(dst, src, mv, rs, rs_ok, dst_ok, c, j):
                dve.wait_ge(rs_ok.sem, rs_ok.at(c, 1))
                nc.vector.tensor_scalar(dst[:, j, :], src[:, j, :], mv[:, j, 0:1], rs[:, j, :],
                                        ALU.subtract, ALU.mult).then_inc(dst_ok.sem, 1)

            def row_max(g, j, h):
                done = -(-(h + 1) * M * M1 // LC)
                dve.wait_ge(lg_ev.sem, lg_ev.at(g, KL * j + done))
                nc.vector.tensor_reduce(nmax[:, j, h * M:(h + 1) * M],
                                        lg[:, j, h * M * M1:(h + 1) * M * M1].rearrange("p (r k) -> p r k", k=M1),
                                        AX_X, ALU.max, negate=True).then_inc(nmax_ok.sem, 1)

            def row_sum(e, j, h):
                if h == 0:
                    dve.wait_ge(exp_ok.sem, exp_ok.at(e, j + 1))
                nc.vector.tensor_reduce(zs[:, j, h * M:(h + 1) * M],
                                        ex[:, j, h * M * M1:(h + 1) * M * M1].rearrange("p (r k) -> p r k", k=M1),
                                        AX_X, ALU.add).then_inc(zs_ok.sem, 1)

            def row_inverse(e, j):
                dve.wait_ge(zs_ok.sem, zs_ok.at(e, H * (j + 1)))
                if not is_first(e):
                    dve.wait_ge(norm_ok.sem, norm_ok.at(e - 1, 2 * j + 2))
                nc.vector.reciprocal(rz[:, j, :], zs[:, j, :]).then_inc(rz_ok.sem, 1)

            def row_value(e, j):
                dve.wait_ge(rz_ok.sem, rz_ok.at(e, j + 1))
                nc.vector.tensor_tensor(rv[:, j, :], rz[:, j, :], vv[:, j, :], ALU.mult).then_inc(rv_ok.sem, 1)

            def scan_products(s, t):
                if t % TS == 0:
                    j = t // TS
                    dve.wait_ge(g_ld[j].sem, g_ld[j].at(s, 32))
                    if not is_first(s):
                        dve.wait_ge(y_st[j].sem, y_st[j].at(s, 0))
                if not (is_first(s) and t == 0):
                    dve.wait_ge(scan.sem, scan.at(s, STEP_INCS * t))
                nc.vector.tensor_tensor(
                    prod[:, :].rearrange("p (i k) -> p i k", k=M1),
                    gates[:, t, :].rearrange("p (i k) -> p i k", k=M1),
                    state[:, (t - 1) % CS, :].unsqueeze(1).broadcast_to([P, HALF, M1]), ALU.mult).then_inc(scan.sem, 1)

            def scan_sums(s, t):
                dve.wait_ge(scan.sem, scan.at(s, STEP_INCS * t + 1))
                nc.vector.tensor_reduce(state[:, t, 1:1 + HALF], prod[:, :].rearrange("p (i k) -> p i k", k=M1),
                                        AX_X, ALU.add).then_inc(scan.sem, 1)

            def scan_exchange(s, t):
                dve.wait_ge(scan.sem, scan.at(s, STEP_INCS * t + 2))
                nc.vector.tensor_copy(state[0:BH, t, 1 + HALF:M1], state[BH:2 * BH, t, 1:1 + HALF]).then_inc(scan.sem, 1)
                nc.vector.tensor_copy(state[BH:2 * BH, t, 1 + HALF:M1], state[0:BH, t, 1:1 + HALF]).then_inc(scan.sem, 1)

            def router_ranks(p, n):
                other = rl[:, :, :].unsqueeze(2).broadcast_to([P, TILES, E, E])
                own = rl[:, :, :].unsqueeze(3).broadcast_to([P, TILES, E, E])
                if n == 0:
                    dve.wait_ge(r_ps.sem, r_ps.at(p, 1))
                    nc.vector.tensor_tensor(rl[:, :, :],
                                            ps[:, 6, 0:N].rearrange("p (j c) -> p j c", j=TILES)[:, :, 0:E],
                                            rb[:, :].unsqueeze(1).broadcast_to([P, TILES, E]), ALU.add
                                            ).then_inc(rank_in.sem, 1)
                elif n == 1:
                    dve.wait_ge(rank_in.sem, rank_in.at(p, 1))
                    nc.vector.tensor_reduce(rmx[:, :], rl[:, :, :], AX_X, ALU.max).then_inc(rank_in.sem, 1)
                    nc.vector.tensor_tensor(req[:, :, :, :], other, own, ALU.is_equal).then_inc(rank_in.sem, 1)
                elif n == 2:
                    dve.wait_ge(rank_in.sem, rank_in.at(p, 3))
                    nc.vector.tensor_tensor(rdl[:, :, :], rl[:, :, :], rmx[:, :].unsqueeze(2).broadcast_to([P, TILES, E]),
                                            ALU.subtract).then_inc(rank_in.sem, 1)
                    nc.vector.tensor_tensor(req[:, :, :, :], req[:, :, :, :],
                                            lower[:, :, :].unsqueeze(1).broadcast_to([P, TILES, E, E]), ALU.mult
                                            ).then_inc(rank_in.sem, 1)
                elif n == 3:
                    nc.vector.tensor_tensor(rgt[:, :, :, :], other, own, ALU.is_gt).then_inc(rank_in.sem, 1)
                else:
                    dve.wait_ge(rank_in.sem, rank_in.at(p, 6))
                    nc.vector.tensor_tensor(rgt[:, :, :, :], rgt[:, :, :, :], req[:, :, :, :], ALU.add
                                            ).then_inc(rank_in.sem, 1)

            def combine_weights(m, n):
                if n == 0:
                    dve.wait_ge(rank_in.sem, rank_in.at(m, 7))
                    nc.vector.tensor_reduce(rank[:, :, :], rgt[:, :, :, :], AX_X, ALU.add).then_inc(weigh.sem, 1)
                elif n == 1:
                    dve.wait_ge(weigh.sem, weigh.at(m, 1))
                    dve.wait_ge(rex_ok.sem, rex_ok.at(m, 1))
                    nc.vector.scalar_tensor_tensor(out=rsl[:, :, :].rearrange("p j e -> p (j e)"),
                                                   in0=rank[:, :, :].rearrange("p j e -> p (j e)"), scalar=TOP_K - 0.5,
                                                   in1=rex[:, :, :].rearrange("p j e -> p (j e)"), op0=ALU.is_lt,
                                                   op1=ALU.mult).then_inc(weigh.sem, 1)
                elif n == 2:
                    dve.wait_ge(weigh.sem, weigh.at(m, 2))
                    nc.vector.tensor_reduce(rsum[:, :], rsl[:, :, :], AX_X, ALU.add).then_inc(weigh.sem, 1)
                elif n == 3:
                    dve.wait_ge(weigh.sem, weigh.at(m, 3))
                    nc.vector.reciprocal(rrec[:, :], rsum[:, :]).then_inc(weigh.sem, 1)
                else:
                    dve.wait_ge(weigh.sem, weigh.at(m, 4))
                    if not is_first(m):
                        dve.wait_ge(weighted_ok.sem, weighted_ok.at(m - 1, E))
                    nc.vector.tensor_tensor(comb[:, :, :], rsl[:, :, :], rrec[:, :].unsqueeze(2).broadcast_to([P, TILES, E]),
                                            ALU.mult).then_inc(weigh.sem, 1)

            def clamp_up(m, k):
                dve.wait_ge(up_ok.sem, up_ok.at(m, k + 1))
                nc.vector.tensor_scalar(up[:, k % 2, :], up[:, k % 2, :], 1.0 + LIMIT, 1.0 - LIMIT,
                                        ALU.min, ALU.max).then_inc(clamp_ok.sem, 1)

            def hidden(m, k, q):
                if q == 0:
                    dve.wait_ge(sg_ok.sem, sg_ok.at(m, k + 1))
                    dve.wait_ge(clamp_ok.sem, clamp_ok.at(m, k + 1))
                    if k >= 2:
                        dve.wait_ge(dn_done.sem, dn_done.at(m, k - 1))
                    elif not is_first(m):
                        dve.wait_ge(dn_done.sem, dn_done.at(m - 1, E + k - 1))
                cols = slice(q * N, (q + 1) * N)
                nc.vector.scalar_tensor_tensor(out=act_t[:, k % 2, cols], in0=sg[:, k % 2, cols], scalar=SILU_LIMIT,
                                               in1=up[:, k % 2, cols], op0=ALU.min, op1=ALU.mult).then_inc(act_ok.sem, 1)

            def aggregate(st, mv, st_ok, mv_ok, c, j):
                dve.wait_ge(st_ok.sem, st_ok.at(c, j + 1))
                dve.sem_inc(passed_dve, 1)
                nc.vector.bn_aggr(mv[:, j, :], st[:, j, :]).then_inc(mv_ok.sem, 1)

            def between(k, n, a, g, e, p, m):
                if m is not None:
                    if n == 3:
                        clamp_up(m, k)
                    if n == 5:
                        hidden(m, k, 0)
                    if n == 6:
                        hidden(m, k, 1)
                if e is not None:
                    if k == 0 and n in (8, 9, 10, 11):
                        row_sum(e, 0, n - 8)
                    if k == 1 and n in (0, 1, 2, 4):
                        row_sum(e, 0, 4 + min(n, 3))
                    if k == 1 and n == 9:
                        row_inverse(e, 0)
                    if k == 1 and n == 11:
                        row_value(e, 0)
                    if k == 2 and n in (0, 1, 2, 4, 7, 8, 9, 10):
                        row_sum(e, 1, (0, 1, 2, 4, 7, 8, 9, 10).index(n))
                    if k == 3 and n == 0:
                        row_inverse(e, 1)
                    if k == 3 and n == 2:
                        row_value(e, 1)
                if g is not None:
                    if k == 3 and n in (4, 7, 8, 9):
                        row_max(g, 0, (4, 7, 8, 9).index(n))
                    if k == 4 and n in (0, 1, 2, 4):
                        row_max(g, 0, 4 + (0, 1, 2, 4).index(n))
                    if k == 5 and n in (4, 9, 10, 11):
                        row_max(g, 1, (4, 9, 10, 11).index(n))
                    if k == 6 and n in (0, 1, 2, 4):
                        row_max(g, 1, 4 + (0, 1, 2, 4).index(n))
                if a is not None:
                    if k == 1 and n in (7, 8):
                        dve.wait_ge(x_in[n - 7].sem, x_in[n - 7].at(a, 16))
                        nc.vector.bn_stats(st1[:, n - 7, :], xg[:, n - 7, :]).then_inc(st1_ok.sem, 1)
                    if k == 1 and n == 10:
                        for j in range(TILES):
                            aggregate(st1, mv1, st1_ok, mv1_ok, a, j)
                    if k == 2 and n == 11:
                        for j in range(TILES):
                            normalise(xh, xg, mv1, rs1, rs1_ok, xh_ok, a, j)
                if p is not None:
                    if k == 3 and n in (10, 11):
                        dve.wait_ge(o_ps.sem, o_ps.at(p, 1))
                        nc.vector.tensor_tensor(go[:, n - 10, :], bank_a(n - 10), mod[:, 2, :], ALU.mult
                                                ).then_inc(go_ok.sem, 1)
                    if k == 4 and n in (9, 10):
                        dve.wait_ge(xn_ok.sem, xn_ok.at(p, 1))
                        nc.vector.bn_stats(st2[:, n - 9, :], xn[:, n - 9, :]).then_inc(st2_ok.sem, 1)
                    if k == 5 and n == 0:
                        for j in range(TILES):
                            aggregate(st2, mv2, st2_ok, mv2_ok, p, j)
                    if k == 5 and n in (7, 8):
                        normalise(xh2, xn, mv2, rs2, rs2_ok, xh2_ok, p, n - 7)
                    if k == 7 and n in (4, 7, 8, 9, 10):
                        router_ranks(p, (4, 7, 8, 9, 10).index(n))
                if m is not None and k == 0 and n in (0, 1, 2, 4, 7):
                    combine_weights(m, (0, 1, 2, 4, 7).index(n))

            def run(a, g, e, s, p, m, o):
                for t in range(CS):
                    k, n = t // (CS // E), 3 * (t % (CS // E))
                    if s is not None:
                        scan_products(s, t)
                    between(k, n, a, g, e, p, m)
                    if s is not None:
                        scan_sums(s, t)
                    between(k, n + 1, a, g, e, p, m)
                    if s is not None:
                        scan_exchange(s, t)
                    between(k, n + 2, a, g, e, p, m)
                if p is not None:
                    dve.wait_ge(h2t_next_ok.sem, h2t_next_ok.at(p, 1))
                    if m is not None:
                        dve.wait_ge(gu_done.sem, gu_done.at(m, 2 * E))
                    nc.vector.tensor_copy(h2t[:, :], h2t_next[:, :]).then_inc(h2t_ok.sem, 1)

            whole(dve, run)

        @block.tensor
        def _(pe):
            pe.wait_ge(consts, CONSTS)
            pe.wait_ge(c_step, 4)
            nc.tensor.transpose(ps[:, 5, 0:B], c_rows[:, :], ident[0:B, 0:B]).then_inc(c_t, 1)
            pe.wait_ge(c_step, 5)
            pe.wait_ge(in_wmod, 16)
            nc.tensor.matmul(ps[:, 6, :], c_tok[:, :], wmod_sb[:, 0:512], start=True, stop=True).then_inc(mod_ps, 1)
            nc.tensor.matmul(ps[:, 7, 0:6 * D - 512], c_tok[:, :], wmod_sb[:, 512:6 * D], start=True,
                             stop=True).then_inc(mod_ps, 1)
            for n in range(N_GROUPS):
                bank = n % 6
                if n >= 6:
                    if n % 2 == 0:
                        pe.wait_ge(w_ev_act, (n - 6) // 2 + 1)
                    else:
                        pe.wait_ge(w_ev_dve, (n - 6) // 2 + 1)
                if n == 0:
                    pe.wait_ge(in_wa, 16)
                    pe.wait_ge(in_small, 16 * 6)
                    nc.tensor.transpose(ps[:, 0, 0:P], wa_rows[:, 0, :], ident[:, :])
                    nc.tensor.transpose(ps[:, 0, P:2 * P], wv_rows[:, :], ident[:, :])
                    nc.tensor.transpose(ps[:, 0, 2 * P:3 * P], wo_rows[:, :], ident[:, :])
                    last = nc.tensor.transpose(ps[:, 0, 3 * P:3 * P + E], rw_rows[:, :], ident[0:E, 0:E])
                elif n < N_WA:
                    for q in range(4):
                        last = nc.tensor.transpose(ps[:, bank, q * P:(q + 1) * P],
                                                   wa_rows[:, WA_GROUPS[n - 1][0] + q, :], ident[:, :])
                elif n < N_WA + E:
                    if n == N_WA:
                        pe.wait_ge(in_gu, 16)
                    for q in range(2 * KI):
                        last = nc.tensor.transpose(ps[:, bank, q * P:(q + 1) * P],
                                                   gu_rows[:, 2 * KI * (n - N_WA) + q, :], ident[:, :])
                elif n < N_GROUPS - 1:
                    if n == N_WA + E:
                        pe.wait_ge(in_dn, 16)
                    for q in range(4):
                        ee = (4 * (n - N_WA - E) + q) // KI
                        last = nc.tensor.transpose(ps[:, bank, q * P:(q + 1) * P],
                                                   dn_rows[:, ee, (q % KI) * P:(q % KI + 1) * P], ident[:, :])
                else:
                    last = nc.tensor.transpose(ps[:, bank, 0:E * 2 * KI], gub_rows[:, :],
                                               ident[0:E * 2 * KI, 0:E * 2 * KI])
                last.then_inc(w_ps, 1)
            pe.wait_ge(w_ev_act, (N_GROUPS + 1) // 2)
            pe.wait_ge(w_ev_dve, N_GROUPS // 2)
            pe.wait_ge(mod_ready, 1)

            def logits(g, n):
                j, k = n // KL, n % KL
                if n == 0:
                    pe.wait_ge(ht_ok.sem, ht_ok.at(g, 1))
                if n >= 2:
                    pe.wait_ge(lg_ev.sem, lg_ev.at(g, n - 1))
                elif not is_first(g):
                    pe.wait_ge(lg_ev.sem, lg_ev.at(g - 1, TILES * KL + n - 1))
                w = min(LC, NL - k * LC)
                nc.tensor.matmul(ps[:, n % 2, 0:w], ht[:, j * P:(j + 1) * P], wl[:, k * LC:k * LC + w], start=True,
                                 stop=True).then_inc(lg_ps.sem, 1)

            def gate_up(m, k):
                if k == 0:
                    pe.wait_ge(h2t_ok.sem, h2t_ok.at(m, 1))
                if k >= 2:
                    pe.wait_ge(up_ok.sem, up_ok.at(m, k - 1))
                elif not is_first(m):
                    pe.wait_ge(up_ok.sem, up_ok.at(m - 1, E + k - 1))
                for which in range(2):
                    for q in range(KI):
                        last = nc.tensor.matmul(gu_ps(k, which)[:, q * N:(q + 1) * N],
                                                wgu[:, k, which * I + q * P:which * I + (q + 1) * P], h2t[:, :],
                                                start=True, stop=True)
                    last.then_inc(gu_done.sem, 1)

            def down(m, k):
                pe.wait_ge(act_ok.sem, act_ok.at(m, KI * (k + 1)))
                if k >= 1:
                    pe.wait_ge(weighted_ok.sem, weighted_ok.at(m, k))
                elif not is_first(m):
                    pe.wait_ge(weighted_ok.sem, weighted_ok.at(m - 1, E))
                for j in range(TILES):
                    for q in range(KI):
                        last = nc.tensor.matmul(dn_ps(j), act_t[:, k % 2, q * N + j * P:q * N + (j + 1) * P],
                                                wd[:, k, q, :], start=(q == 0), stop=(q == KI - 1))
                last.then_inc(dn_done.sem, 1)

            def run(a, g, e, s, p, m, o):
                for k in range(E):
                    if m is not None:
                        gate_up(m, k)
                    if g is not None and k < KL:
                        logits(g, 2 * k)
                    if m is not None and k == 1:
                        pe.wait_ge(weigh.sem, weigh.at(m, 5))
                        for j in range(TILES):
                            last = nc.tensor.transpose(bank_a(j)[0:E, :], comb[:, j, :], ident[:, :])
                        last.then_inc(combt_ps.sem, 1)
                        down(m, 0)
                        pe.wait_ge(combt_ok.sem, combt_ok.at(m, 1))
                        for j in range(TILES):
                            last = nc.tensor.matmul(bank_a(j), combt[:, j * P:(j + 1) * P], bd[:, :], start=True, stop=True)
                        last.then_inc(b_ps.sem, 1)
                    if m is not None and k >= 2:
                        down(m, k - 1)
                    if g is not None and k < KL:
                        logits(g, 2 * k + 1)
                    if p is not None and k == 2:
                        if m is not None:
                            pe.wait_ge(bias_ok.sem, bias_ok.at(m, 1))
                        elif a is not None or g is not None:
                            pe.wait_ge(ht_ok.sem, ht_ok.at(g, 1))
                        for j in range(TILES):
                            pe.wait_ge(y_ld[j].sem, y_ld[j].at(p, 16 * B))
                            last = nc.tensor.transpose(bank_a(j), yt_tok[:, j, :], ident[:, :])
                        last.then_inc(yt_ps.sem, 1)
                    if p is not None and k == 3:
                        pe.wait_ge(yt_ok.sem, yt_ok.at(p, 1))
                        for j in range(TILES):
                            last = nc.tensor.matmul(bank_a(j), yt[:, j * P:(j + 1) * P], wo[:, :], start=True, stop=True)
                        last.then_inc(o_ps.sem, 1)
                    if a is not None and k == 5:
                        if p is not None:
                            pe.wait_ge(go_ok.sem, go_ok.at(p, TILES))
                        elif not is_first(a):
                            pe.wait_ge(ht_ok.sem, ht_ok.at(a - 1, 1))
                        pe.wait_ge(h_ok.sem, h_ok.at(a, 1))
                        for j in range(TILES):
                            last = nc.tensor.transpose(bank_a(j), hh[:, j, :], ident[:, :])
                        last.then_inc(ht_ps.sem, 1)
                    if p is not None and k == 6:
                        if a is not None:
                            pe.wait_ge(ht_ok.sem, ht_ok.at(a, 1))
                        else:
                            pe.wait_ge(go_ok.sem, go_ok.at(p, TILES))
                        pe.wait_ge(h2_ok.sem, h2_ok.at(p, 1))
                        for j in range(TILES):
                            last = nc.tensor.transpose(bank_a(j), h2[:, j, :], ident[:, :])
                        last.then_inc(h2t_ps.sem, 1)
                    if p is not None and k == 7:
                        pe.wait_ge(h2t_next_ok.sem, h2t_next_ok.at(p, 1))
                        for j in range(TILES):
                            last = nc.tensor.matmul(bank_a(j)[:, 0:E], h2t_next[:, j * P:(j + 1) * P], rw[:, :],
                                                    start=True, stop=True)
                        last.then_inc(r_ps.sem, 1)
                if m is not None:
                    down(m, E - 1)

            whole(pe, run)


_INS = ['L0_attn_x', 'L0_attn_norm_w', 'L0_attn_W_v', 'L0_attn_W_a', 'L0_attn_W_out', 'L0_ffn_router_weight',
        'L0_ffn_router_bias', 'L0_ffn_gate_up_proj', 'L0_ffn_gate_up_proj_bias', 'L0_ffn_down_proj',
        'L0_ffn_down_proj_bias', 'L0_c', 'L0_wmod']
_OUTS = [((8, 512, 128), 'float32')]


def kernel(**inputs):
    import numpy as _np
    import concourse.bacc as _bacc
    from concourse import mybir as _mybir
    from concourse.bass_utils import run_bass_kernel_spmd as _run

    nc = _bacc.Bacc("TRN2", target_bir_lowering=False, num_devices=1)
    arrays, args = {}, []
    for name in _INS:
        a = _np.ascontiguousarray(inputs[name])
        arrays[f"in_{name}_dram"] = a
        args.append(nc.dram_tensor(f"in_{name}_dram", a.shape, _mybir.dt.from_np(a.dtype), kind="ExternalInput").ap())
    for i, (shape, dtype) in enumerate(_OUTS):
        dt = _mybir.dt.from_np(_np.dtype(dtype))
        args.append(nc.dram_tensor(f"out_{i}_dram", shape, dt, kind="ExternalOutput").ap())
    adaln_block(nc, *args)
    r = _run(nc, [arrays], core_ids=[0])
    got = tuple(r.results[0][f"out_{i}_dram"] for i in range(len(_OUTS)))
    return got[0]
```
